# Optimizing a Trainium2 kernel written in Bass

```python
import numpy as np
import jax
import jax.numpy as jnp

def _softmax(x, axis=-1):
    return jax.nn.softmax(x, axis=axis)

def _gelu(x):
    return jax.nn.gelu(x, approximate=True)

def _silu(x):
    return jax.nn.silu(x)

def _sigmoid(x):
    return jax.nn.sigmoid(x)

def _layernorm(x, axis=-1, eps=1e-05):
    m = jnp.mean(x, axis=axis, keepdims=True)
    v = jnp.var(x, axis=axis, keepdims=True)
    return (x - m) / jnp.sqrt(v + eps)

def _scatter_add(tgt, idx, src, axis=0):
    return tgt.at[idx].add(src)

def _segment_sum(src, seg, n):
    return jax.ops.segment_sum(src, seg, n)
kernel_name = 'mk_flamingo_gated_d1_seqx_r8_c02e26'

def setup_inputs(seed: int=0):
    np.random.seed(seed)
    _w = jnp.asarray

    def _rec_inputs():
        import jax
        import jax.numpy as jnp
        _rk = jax.random.key(seed)
        x = -0.0002928 + 1 * jax.random.normal(jax.random.fold_in(_rk, 1), (8, 128, 256), jnp.float32)
        _lenS = 128 - jax.random.randint(jax.random.fold_in(_rk, 7), (8,), 0, max(1, 128 // 4) + 1, jnp.int32)
        _lenS2 = 128 - jax.random.randint(jax.random.fold_in(_rk, 8), (8,), 0, max(1, 128 // 4) + 1, jnp.int32)
        _ctx_2048P = jax.random.normal(jax.random.fold_in(_rk, 11), (8, 16, 256), jnp.float32)
        _ctx_2048c = jax.random.dirichlet(jax.random.fold_in(_rk, 511), 0.3 * jnp.ones((16,), jnp.float32), (8, 128))
        _ctx_2048t = jnp.einsum('bsk,bkd->bsd', _ctx_2048c, _ctx_2048P)
        _ctx_2048t = _ctx_2048t * jax.lax.rsqrt(jnp.mean(jnp.square(_ctx_2048t)) + 1e-12) * 0.953939
        ctx_2048 = -1.39393e-06 + 0.999914 * (_ctx_2048t + 0.3 * jax.random.normal(jax.random.fold_in(_rk, 611), (8, 128, 256), jnp.float32))
        _validS = jnp.arange(128)[None, :] < _lenS[:, None]
        _validS2 = jnp.arange(128)[None, :] < _lenS2[:, None]
        _causal = jnp.tril(jnp.ones((128, 128), dtype=bool))
        mask_Bx1x2048_fk1 = jnp.where(jnp.ones((8, 1, 256), dtype=bool), 1.0, 0.0).astype(jnp.float32)
        _g = jax.random.normal(jax.random.fold_in(_rk, 9001), (2, 1), jnp.float32)
        _g = jnp.sign(_g) * jnp.maximum(jnp.abs(_g), 1.0) + (_g == 0) * 1.0
        g_xattn = _g[0]
        g_ffn = _g[1]
        return (x, ctx_2048, mask_Bx1x2048_fk1, g_xattn, g_ffn)
    x, ctx_2048, mask_Bx1x2048_fk1, g_xattn, g_ffn = _rec_inputs()

    def _L0_xattn_setup():
        import math
        import jax, jax.numpy as jnp
        import numpy as np
        SIZE = 128
        HEADS = 16
        HEAD_DIM = SIZE // HEADS
        B, T, S = (2, 256, 256)
        NEG = 1000000.0
        key = jax.random.key(seed)
        ks = jax.random.split(key, 10)
        target = jax.random.normal(ks[0], (B, SIZE, T), dtype=jnp.float32)
        source = jax.random.normal(ks[1], (B, SIZE, S), dtype=jnp.float32)
        target_mask = (jax.random.uniform(ks[2], (B, 1, T)) > 0.1).astype(jnp.float32)
        source_mask = (jax.random.uniform(ks[3], (B, 1, S)) > 0.1).astype(jnp.float32)
        scale = 1.0 / math.sqrt(SIZE)
        Wq = jax.random.normal(ks[4], (SIZE, SIZE), dtype=jnp.float32) * scale
        Wk = jax.random.normal(ks[5], (SIZE, SIZE), dtype=jnp.float32) * scale
        Wv = jax.random.normal(ks[6], (SIZE, SIZE), dtype=jnp.float32) * scale
        bq = jax.random.normal(ks[7], (SIZE,), dtype=jnp.float32) * 0.01
        bk = jax.random.normal(ks[8], (SIZE,), dtype=jnp.float32) * 0.01
        bv = jax.random.normal(ks[9], (SIZE,), dtype=jnp.float32) * 0.01
        return {'target': target, 'source': source, 'target_mask': target_mask, 'source_mask': source_mask, 'Wq': Wq, 'bq': bq, 'Wk': Wk, 'bk': bk, 'Wv': Wv, 'bv': bv}
    _L0_xattn_all = _L0_xattn_setup()
    _L0_xattn_in = {k: v for k, v in _L0_xattn_all.items() if k in ('Wq', 'bq', 'Wk', 'bk', 'Wv', 'bv')}
    del _L0_xattn_all

    def _L0_ffn_setup():
        import jax, jax.numpy as jnp
        import numpy as np
        B, S, H = (2, 64, 256)
        E, I, K = (64, 176, 6)
        NS = 2
        SH_I = I * NS
        key = jax.random.key(seed)
        ks = jax.random.split(key, 6)
        s = 0.02
        return {'hidden_states': jax.random.normal(ks[0], (B, S, H), jnp.float32), 'gate_w': jax.random.normal(ks[1], (E, H), jnp.float32) * s, 'experts_w1': jax.random.normal(ks[2], (E, I, H), jnp.float32) * s, 'experts_w2': jax.random.normal(ks[3], (E, H, I), jnp.float32) * s, 'shared_gate_up': jax.random.normal(ks[4], (2 * SH_I, H), jnp.float32) * s, 'shared_down': jax.random.normal(ks[5], (H, SH_I), jnp.float32) * s}
    _L0_ffn_all = _L0_ffn_setup()
    _L0_ffn_in = {k: v for k, v in _L0_ffn_all.items() if k in ('gate_w', 'experts_w1', 'experts_w2', 'shared_gate_up', 'shared_down')}
    del _L0_ffn_all
    return {'x': x, 'ctx_2048': ctx_2048, 'mask_Bx1x2048_fk1': mask_Bx1x2048_fk1, 'g_xattn': g_xattn, 'g_ffn': g_ffn, 'L0_xattn_Wq': _L0_xattn_in['Wq'], 'L0_xattn_bq': _L0_xattn_in['bq'], 'L0_xattn_Wk': _L0_xattn_in['Wk'], 'L0_xattn_bk': _L0_xattn_in['bk'], 'L0_xattn_Wv': _L0_xattn_in['Wv'], 'L0_xattn_bv': _L0_xattn_in['bv'], 'L0_ffn_gate_w': _L0_ffn_in['gate_w'], 'L0_ffn_experts_w1': _L0_ffn_in['experts_w1'], 'L0_ffn_experts_w2': _L0_ffn_in['experts_w2'], 'L0_ffn_shared_gate_up': _L0_ffn_in['shared_gate_up'], 'L0_ffn_shared_down': _L0_ffn_in['shared_down']}

def reference(x, ctx_2048, mask_Bx1x2048_fk1, g_xattn, g_ffn, L0_xattn_Wq, L0_xattn_bq, L0_xattn_Wk, L0_xattn_bk, L0_xattn_Wv, L0_xattn_bv, L0_ffn_gate_w, L0_ffn_experts_w1, L0_ffn_experts_w2, L0_ffn_shared_gate_up, L0_ffn_shared_down):
    import jax
    import jax.numpy as jnp

    def _L0_xattn_ref(target, source, target_mask, source_mask, Wq, bq, Wk, bk, Wv, bv):
        import math
        import jax, jax.numpy as jnp
        import numpy as np
        SIZE = 128
        HEADS = 16
        HEAD_DIM = SIZE // HEADS
        B, T, S = (2, 256, 256)
        NEG = 1000000.0
        b, _, t = target.shape
        s = source.shape[-1]
        q = jnp.einsum('oc,bct->bot', Wq, target) + bq[None, :, None]
        k = jnp.einsum('oc,bcs->bos', Wk, source) + bk[None, :, None]
        v = jnp.einsum('oc,bcs->bos', Wv, source) + bv[None, :, None]
        q = q.reshape(b, HEADS, HEAD_DIM, t)
        k = k.reshape(b, HEADS, HEAD_DIM, s)
        v = v.reshape(b, HEADS, HEAD_DIM, s)
        dot = jnp.einsum('bhdt,bhds->bhts', q, k) / math.sqrt(HEAD_DIM)
        mask = target_mask[:, :, :, None] * source_mask[:, :, None, :]
        dot = mask * dot - (1.0 - mask) * NEG
        amap = jax.nn.softmax(dot, axis=-1) * mask
        out = jnp.einsum('bhts,bhds->bhdt', amap, v)
        return out.reshape(b, HEADS * HEAD_DIM, t)

    def _L0_ffn_ref(hidden_states, gate_w, experts_w1, experts_w2, shared_gate_up, shared_down):
        import jax, jax.numpy as jnp
        import numpy as np
        B, S, H = (2, 64, 256)
        E, I, K = (64, 176, 6)
        NS = 2
        SH_I = I * NS
        orig_shape = hidden_states.shape
        x = hidden_states.reshape(-1, orig_shape[-1])
        router_logits = x @ gate_w.T
        probs = jax.nn.softmax(router_logits, axis=-1)
        topk_w, topk_idx = jax.lax.top_k(probs, K)
        topk_w = topk_w / jnp.sum(topk_w, axis=-1, keepdims=True)
        combine = jnp.sum(jax.nn.one_hot(topk_idx, E, dtype=x.dtype) * topk_w[..., None], axis=1)
        h = jax.nn.silu(jnp.einsum('th,eih->tei', x, experts_w1))
        y = jnp.einsum('tei,ehi->teh', h, experts_w2)
        routed_out = jnp.einsum('teh,te->th', y, combine)
        gu = x @ shared_gate_up.T
        g, u = jnp.split(gu, 2, axis=-1)
        shared_out = jax.nn.silu(g) * u @ shared_down.T
        return (routed_out + shared_out).reshape(orig_shape)
    x = x + jnp.tanh(g_xattn[0]) * _L0_xattn_ref(_layernorm(x, axis=-1), ctx_2048, mask_Bx1x2048_fk1, mask_Bx1x2048_fk1, L0_xattn_Wq, L0_xattn_bq, L0_xattn_Wk, L0_xattn_bk, L0_xattn_Wv, L0_xattn_bv)
    x = x + jnp.tanh(g_ffn[0]) * _L0_ffn_ref(_layernorm(x, axis=-1), L0_ffn_gate_w, L0_ffn_experts_w1, L0_ffn_experts_w2, L0_ffn_shared_gate_up, L0_ffn_shared_down)
    return x

_drawn_inputs = setup_inputs


def setup_inputs(seed=0):
    import zlib

    import numpy as np

    out = dict(_drawn_inputs(seed))
    spreads = {}
    factors = {'L0_xattn_bq': 25.259,
     'L0_xattn_bk': 64.0,
     'L0_xattn_bv': 6.847,
     'L0_ffn_gate_w': 3.377,
     'L0_ffn_experts_w1': 3.082,
     'L0_ffn_experts_w2': 3.074,
     'L0_ffn_shared_gate_up': 3.11,
     'L0_ffn_shared_down': 3.103}
    for name, (base, spread) in spreads.items():
        noise = np.random.default_rng([zlib.crc32(name.encode()), seed]).standard_normal(out[name].shape)
        drawn = base * np.exp(spread * noise) if base else spread * noise
        out[name] = jnp.asarray(drawn.astype(out[name].dtype))
    for name, factor in factors.items():
        out[name] = (out[name] * factor).astype(out[name].dtype)
    return out
```

```python
import concourse.bass as bass
from concourse import mybir
from contextlib import ExitStack


def build_gated_block(nc, x, ctx_in, mask, g_xattn, g_ffn, wq, bq, wk, bk, wv, bv, gate, w1, w2, sgu, sd, out):
    F32, F32R, F16, U32, I32 = (mybir.dt.float32, mybir.dt.float32r, mybir.dt.float16, mybir.dt.uint32,
                                mybir.dt.int32)
    ALU, ACT, AX = mybir.AluOpType, mybir.ActivationFunctionType, mybir.AxisListType

    P = 128
    B, T = x.shape[1], x.shape[2]
    H, D = 16, 8
    TC = T // P
    E = gate.shape[2]
    K = 6
    NT = B * P
    IC = sd.shape[0]
    EPS = 1e-5
    NEG = 1000000.0
    ROOT = float(D) ** 0.5
    HD1 = D + 1
    PART = 2 * HD1
    SROWS = 2 * PART
    AROWS = 96
    BROWS = AROWS + 2
    FAR = 8192

    es = ExitStack()
    with es:
        def sb(name, shape, dt=F32):
            return es.enter_context(nc.sbuf_tensor(name, shape, dt))

        def sem(name):
            return es.enter_context(nc.semaphore(name))

        q_parts = nc.dram_tensor("q_parts", [B, 2, HD1 * H, T], F32).ap()
        k_parts = nc.dram_tensor("k_parts", [B, 2, HD1 * H, T], F32).ap()
        max_parts = nc.dram_tensor("max_parts", [B, 2, H, T], F32).ap()
        tokens = nc.dram_tensor("tokens", [NT, T], F32).ap()
        routed = nc.dram_tensor("routed", [NT * K, T], F32).ap()

        x_sb = sb("x_sb", [P, B, T])
        ctx_sb = sb("ctx_sb", [P, B, T])
        xn = sb("xn", [P, B, T])
        vals = sb("vals", [P, B * TC, P])
        v_pad = sb("v_pad", [P, 2, TC, H, 32])
        probs = sb("probs", [P, 4, 2 * TC * T])
        o_sb = sb("o_sb", [P, 2, 4, T])
        o_n = sb("o_n", [P, TC, P])
        full = sb("full", [P, 2, 2 * T])
        high = sb("high", [P, 2, 2 * T], F32R)
        low = sb("low", [P, 2, 2 * T], F32R)
        w_sb = sb("w_sb", [P, 3, P])
        b_sb = sb("b_sb", [P, 2])
        bv_sb = sb("bv_sb", [P, P])
        mask_bc = sb("mask_bc", [P, B * T])
        mask_r = sb("mask_r", [B * TC, P])
        mask_c = sb("mask_c", [P, B * TC])
        mask_b = sb("mask_b", [B, T])
        mask_k = sb("mask_k", [B, T])
        mask_hl = sb("mask_hl", [B, 4, T], F32R)
        ident = sb("ident", [P, P])
        zeros = sb("zeros", [P, 1])
        ones_st = sb("ones_st", [2, T])
        stats = sb("stats", [P, B, 6])
        mv = sb("mv", [P, B, 2])
        var = sb("var", [P, B])
        rstd = sb("rstd", [P, B])
        neg_half = sb("neg_half", [P, B])
        mx = sb("mx", [P, 2, TC, H])
        nm = sb("nm", [H, 2, 2, T], F32R)
        rz = sb("rz", [P, 2, H])
        g_sb = sb("g_sb", [P, 2])
        tg = sb("tg", [P, 3])
        xt = ctx_sb[:, :, :].rearrange("p b t -> p (b t)").rearrange("p (k n) -> p k n", k=TC)
        gate_sb = sb("gate_sb", [P, TC, E])
        v8 = sb("v8", [P, B, 8])
        i8 = sb("i8", [P, B, 8], U32)
        if8 = sb("if8", [P, B, 8])
        iota_e = sb("iota_e", [P, E])
        route = vals[:, :, :].rearrange("p s n -> p (s n)").bitcast(F16)[:, 0:B * E * 4].rearrange("p (b e n) -> p b e n", b=B, e=E)
        picked = sb("picked", [P, 4, B, 4], F16)
        iota_w = sb("iota_w", [P, NT], F16)
        iota_t = sb("iota_t", [P, B])
        iota_p = sb("iota_p", [P, 1])
        low6 = sb("low6", [P, 1])
        tri = sb("tri", [P, P], F16)
        tri_f = sb("tri_f", [E, E])
        ones16 = sb("ones16", [P, P], F16)
        ones_f = sb("ones_f", [E, 1])
        e6 = sb("e6", [P, B, K])
        e6s = sb("e6s", [P, B])
        ww = sb("ww", [P, B, K])
        n_e = sb("n_e", [E, 1])
        c128 = sb("c128", [E, 7])
        c_tmp = sb("c_tmp", [E, 7])
        extra = sb("extra", [E, 1])
        o_beg = sb("o_beg", [E, 1])
        o_end = sb("o_end", [E, 1])
        NOV = NT * K // (P + 1)
        iota_q = sb("iota_q", [E, NOV])
        t_ge = sb("t_ge", [E, NOV])
        t_in = sb("t_in", [E, NOV])
        t_c = sb("t_c", [E, NOV])
        t_c2 = sb("t_c2", [E, NOV])
        plan = sb("plan", [1, 2 * NOV + 1], I32)

        g_idx = sb("g_idx", [P, 8], U32)
        s_idx = sb("s_idx", [P, 8], U32)

        with ExitStack() as attention:
            q_st, k_st = ([attention.enter_context(nc.sbuf_tensor(f"{name}{n}", [P, H, T], F32R)) for n in range(3)]
                          for name in ("q_st", "k_st"))
        sgu_sb = sb("sgu_sb", [P, TC, 8, IC])
        sd_sb = sb("sd_sb", [IC, 4, T])
        s_h = sb("s_h", [IC, 4, NT])
        s_th = sb("s_th", [IC, 2, 512])
        s_gg = sb("s_gg", [IC, 2, 512])
        w1_sb = sb("w1_sb", [P, 4, TC, 2 * IC])
        w2_sb = sb("w2_sb", [P, 4, 2, T])
        y6 = sb("y6", [P, 2, K, T])
        onehot = sb("onehot", [P, 2, B, P], F16)
        rows = sb("rows", [P, 4, T])
        xe = sb("xe", [P, 2, TC, P])
        th = sb("th", [IC, 2, 2 * P])
        hs = sb("hs", [IC, 2, 2, P])
        y_sb = sb("y_sb", [P, 4, T])
        logits = sb("logits", [P, B, E])
        eq = sb("eq", [P, B, E])
        rank = sb("rank", [P, B, E])
        chosen = sb("chosen", [P, B, E], F16)
        far = sb("far", [P, B, E])

        def ps(name, banks):
            return es.enter_context(nc.psum_tensor(name, [P, 512 * banks], F32))

        b0, b1 = ps("b0", 1), ps("b1", 1)
        score = [ps("score0", 2), ps("score1", 2)]
        b6, b7 = ps("b6", 1), ps("b7", 1)
        bank = [b0[:, :], b1[:, :], score[0][:, 0:512], score[0][:, 512:1024], score[1][:, 0:512],
                score[1][:, 512:1024], b6[:, :], b7[:, :]]

        ld_x, ld_ctx, ld_w, ld_small, ld_mask, ld_bc, ld_gate, ld_shared = [sem(n) for n in (
            "ld_x", "ld_ctx", "ld_w", "ld_small", "ld_mask", "ld_bc", "ld_gate", "ld_shared")]
        consts = sem("consts")
        zeroed = sem("zeroed")
        zero_col = sem("zero_col")
        ones_done = sem("ones_done")
        ones_in = sem("ones_in")
        dv = sem("dv")
        av = sem("av")
        pl = sem("pl")
        pool_steps = sem("pool_steps")
        var_done = sem("var_done")
        rstd_done = sem("rstd_done")
        normed = sem("normed")
        proj = sem("proj")
        taken = sem("taken")
        mask_col = sem("mask_col")
        aug = sem("aug")
        fulls = sem("fulls")
        highs = sem("highs")
        lows = sem("lows")
        parts_out = [sem(f"parts_out{n}") for n in range(B // 2)]
        aug_out = sem("aug_out")
        stack_in = [sem(f"stack_in{n}") for n in range(3)]
        max_out = sem("max_out")
        max_in = sem("max_in")
        a_done, max_done, b_done, exp_done, pv_done, os_done, t_ready, nm_done, v_ready, on_done, x1_done = [
            sem(n) for n in ("a_done", "max_done", "b_done", "exp_done", "pv_done", "os_done", "t_ready",
                             "nm_done", "v_ready", "on_done", "x1_done")]
        tanh_g = sem("tanh_g")
        tok_normed, tok_out, xt_ready, xt_done, lg_ready, lg_done = [sem(n) for n in (
            "tok_normed", "tok_out", "xt_ready", "xt_done", "lg_ready", "lg_done")]
        soft, softd, chosen_done, pos_ready, cnt_ready, beg_in, beg_ready, plan_in, plan_ready, plan_done, route_done = [
            sem(n) for n in ("soft", "softd", "chosen_done", "pos_ready", "cnt_ready", "beg_in", "beg_ready",
                             "plan_in", "plan_ready", "plan_done", "route_done")]
        sg_ready, sth_done, sh_done, sdn_ready, acc_done = [sem(n) for n in (
            "sg_ready", "sth_done", "sh_done", "sdn_ready", "acc_done")]
        pick_done, hot, inv, idx, xpose, xe_done, s1, th_done, hs_done, s2, y_done = [sem(n) for n in (
            "pick_done", "hot", "inv", "idx", "xpose", "xe_done", "s1", "th_done", "hs_done", "s2", "y_done")]
        w_in = [sem(f"w_in{n}") for n in range(4)]
        rows_in = [sem(f"rows_in{n}") for n in range(4)]
        y_out = [sem(f"y_out{n}") for n in range(4)]
        (v_w, v_pick, v_hot, v_inv, v_idx, v_rows, v_x, v_xe, v_s1, v_th, v_hs, v_s2, v_y, v_out, v_free) = [
            sem(f"over_{n}") for n in ("w", "pick", "hot", "inv", "idx", "rows", "x", "xe", "s1", "th", "hs", "s2", "y", "out",
                                       "free")]
        y6_in = [sem(f"y6_in{n}") for n in range(2)]
        scattered, mixed, stored = sem("scattered"), sem("mixed"), sem("stored")

        block = es.enter_context(nc.Block())

        NA = B * H
        LAG = 24
        NP = NA // 2
        NG = NA // 4

        def pair_at(a):
            return (a - LAG) // 2 if a >= LAG and (a - LAG) % 2 == 0 else -1

        def pair_of(a):
            p = pair_at(a)
            return p if 0 <= p < NP else None

        def group_of(a):
            p = pair_at(a)
            return (p - 3) // 2 if p >= 3 and p % 2 == 1 and (p - 3) // 2 < NG else None

        events = {}
        for b in range(B):
            events.setdefault(16 * b + 17, []).append(("max", b, 0))
            events.setdefault(16 * b + 45, []).append(("out", b, 0))
            events.setdefault(16 * b + 47, []).append(("out", b, 1))
            events.setdefault(16 * b + 51, []).append(("back", b, 0))
        STEPS = 16 * (B - 1) + 54
        t_index = {e: n for n, e in enumerate(e for a in sorted(events) for e in events[a])}

        L_PICK, L_HOT, L_INV, L_IDX, L_GATHER, L_X, L_S1 = 8, 7, 7, 6, 5, 3, 2
        U = 8
        LOOP = range(1, 7)

        class Ex:

            def __init__(self, q, r):
                self.q, self.r = q + r // U if r >= U or r < 0 else q, r % U
                self.v = self.q * U + self.r

            def use(self, ring):
                return self.q * (U // ring) + self.r // ring

        def experts(eng, stages):
            def step(q, r, check):
                for lead, f in stages:
                    e = Ex(q, r + lead)
                    if not check or 0 <= e.v < E:
                        f(e)

            for n in range(-L_PICK, U):
                step(0, n, True)
            with eng.Fori(LOOP.start, LOOP.stop) as q:
                for r in range(U):
                    step(q, r, False)
            for n in range(U * LOOP.stop, E):
                step(0, n, True)

        def first(e, n):
            return isinstance(e.v, int) and e.v < n

        @block.sync
        def _(sp):
            sp.dma_start(ctx_sb[:, :, :], ctx_in).then_inc(ld_ctx, 16)
            for n, w in enumerate((wk, wq, wv)):
                sp.dma_start(w_sb[:, n, :], w).then_inc(ld_w, 16)
            sp.dma_start(x_sb[:, :, :], x).then_inc(ld_x, 16)
            sp.dma_start(mask_bc[:, :], mask.rearrange("(o b) t -> o (b t)", o=1).to_broadcast([P, B * T])).then_inc(ld_bc, 16)
            sp.dma_start(gate_sb[:, :, :], gate).then_inc(ld_gate, 16)
            sp.wait_ge(aug, 4)
            for parts, m in ((q_parts, 0), (k_parts, 2)):
                for hl in range(2):
                    dst = parts[:, hl, D * H:HD1 * H, :]
                    sp.dma_start(dst, mask_hl[:, m + hl:m + hl + 1, :].bitcast(F32).to_broadcast([B, H, T])).then_inc(aug_out, 16)
            for j in range(B):
                parts, n = (k_parts, j) if j < B // 2 else (q_parts, j - B // 2)
                for hl, (t, done) in enumerate(((high, highs), (low, lows))):
                    sp.wait_ge(done, j + 1)
                    dst = parts[2 * n:2 * n + 2, hl, 0:D * H, :].rearrange("b p t -> p b t")
                    sp.dma_start(dst, t[:, j % 2, :].bitcast(F32).rearrange("p (b t) -> p b t", b=2)).then_inc(parts_out[n], 16)
            sp.wait_ge(aug_out, 64)
            sp.wait_ge(zeroed, 2)
            sp.wait_ge(ones_done, 1)
            for s in range(3):
                sp.dma_start(k_st[s][AROWS:BROWS, :, :].bitcast(F32),
                             ones_st[:, :].rearrange("p (o t) -> p o t", o=1).to_broadcast([2, H, T])).then_inc(ones_in, 16)

            def load_stacks(b):
                s, use = b % 3, stack_in[b % 3]
                sp.wait_ge(parts_out[b // 2], 64)
                if b >= 3:
                    sp.wait_ge(b_done, 8 * (b - 2))
                qp = q_parts[b].rearrange("l (d h) t -> (l d) (h t)", h=H)
                kp = k_parts[b].rearrange("l (d h) t -> (l d) (h t)", h=H)
                flatq = q_st[s][:, :, :].bitcast(F32).rearrange("p h t -> p (h t)")
                flatk = k_st[s][:, :, :].bitcast(F32).rearrange("p h t -> p (h t)")
                sp.dma_start(flatq[0:PART, :], qp).then_inc(use, 16)
                sp.dma_start(flatq[PART:SROWS, :], qp).then_inc(use, 16)
                sp.dma_start(flatk[0:PART, :], kp).then_inc(use, 16)
                sp.dma_start(flatk[PART:PART + HD1, :], kp[HD1:PART, :]).then_inc(use, 16)
                sp.dma_start(flatk[PART + HD1:SROWS, :], kp[0:HD1, :]).then_inc(use, 16)

            def send_max(b):
                sp.wait_ge(nm_done, 2 * (b + 1))
                for hl in range(2):
                    sp.dma_start(max_parts[b, hl], nm[:, b % 2, hl, :].bitcast(F32)).then_inc(max_out, 16)
                sp.wait_ge(max_out, 32 * (b + 1))
                flatq = q_st[b % 3][:, :, :].bitcast(F32).rearrange("p h t -> p (h t)")
                sp.dma_start(flatq[AROWS:BROWS, :], max_parts[b].rearrange("l h t -> l (h t)")).then_inc(max_in, 16)

            for b in range(3):
                load_stacks(b)
            for b in range(B):
                send_max(b)
                if 1 <= b and b + 2 < B:
                    load_stacks(b + 2)
            sp.wait_ge(b_done, NP)
            sp.dma_start(sgu_sb[:, :, :, :], sgu).then_inc(ld_shared, 16)
            sp.dma_start(sd_sb[:, :, :], sd).then_inc(ld_shared, 16)
            for b in range(B):
                sp.wait_ge(tok_normed, b + 1)
                sp.dma_start(tokens[b * P:(b + 1) * P, :], xn[:, b, :]).then_inc(tok_out, 16)

            def load_weights(e):
                r = e.r % 4
                if not first(e, 4):
                    sp.wait_ge(s2, e.v - 3)
                sp.dma_start(w1_sb[:, r, :, :], w1[bass.ds(e.v, 1)].rearrange("o p k i -> p (o k) i")).then_inc(w_in[r], 16)
                sp.dma_start(w2_sb[:, r, :, :], w2[bass.ds(e.v, 1)].rearrange("o p c t -> p (o c) t")).then_inc(w_in[r], 16)

            experts(sp, [(3, load_weights)])
            sp.wait_ge(plan_done, 1)
            n_over = sp.value_load(plan[0:1, 2 * NOV:2 * NOV + 1], min_val=0, max_val=NOV)
            sp.wait_ge(s2, E)
            with sp.If(n_over > 0):
                with sp.Fori(0, n_over) as i:
                    e = sp.value_load(plan[0:1, bass.ds(i, 1)], min_val=0, max_val=E - 1)
                    sp.wait_ge(v_s2, i + 1)
                    sp.dma_start(w1_sb[:, 0, :, :], w1[bass.ds(e, 1)].rearrange("o p k i -> p (o k) i")).then_inc(v_w, 16)
                    sp.dma_start(w2_sb[:, 0, :, :], w2[bass.ds(e, 1)].rearrange("o p c t -> p (o c) t")).then_inc(v_w, 16)
            with sp.Else():
                sp.nop()
            sp.wait_ge(scattered, 1)
            for b in range(B + 1):
                if b < B:
                    if b >= 2:
                        sp.wait_ge(mixed, b - 1)
                    src = routed[b * P * K:(b + 1) * P * K, :].rearrange("(p k) t -> p k t", k=K)
                    sp.dma_start(y6[:, b % 2, :, :], src).then_inc(y6_in[b % 2], 16)
                if b >= 1:
                    sp.wait_ge(mixed, b)
                    sp.dma_start(out[:, b - 1, :], x_sb[:, b - 1, :]).then_inc(stored, 16)
            sp.wait_ge(stored, 16 * B)

        @block.gpsimd
        def _(pool):
            n = [0]

            def link(ins):
                n[0] += 1
                ins.then_inc(pl, 1)
                pool.wait_ge(pl, n[0])

            pool.memset(zeros[:], 0.0).then_inc(zero_col, 1)
            pool.memset(ones_st[:], 1.0).then_inc(ones_done, 1)
            link(pool.memset(ident[:], 0.0))
            link(pool.affine_select(out=ident[:], in_=ident[:], compare_op=ALU.not_equal, fill=1.0, base=0,
                                    pattern=[[-1, P]], channel_multiplier=1))
            pool.memset(ones16[:], 1.0).then_inc(consts, 1)
            link(pool.memset(tri[:], 1.0))
            link(pool.affine_select(out=tri[:], in_=tri[:], compare_op=ALU.is_gt, fill=0.0, base=0,
                                    pattern=[[1, P]], channel_multiplier=-1))
            link(pool.memset(tri_f[:], 1.0))
            link(pool.affine_select(out=tri_f[:], in_=tri_f[:], compare_op=ALU.is_gt, fill=0.0, base=0,
                                    pattern=[[1, E]], channel_multiplier=-1))
            link(pool.memset(ones_f[:], 1.0))
            link(pool.memset(neg_half[:], -0.5))
            link(pool.memset(v_pad[:, :, :, :, :], 0.0))
            link(pool.memset(v_pad[:, :, :, :, D:D + 1], 1.0))
            pool.iota(iota_e[:], pattern=[[1, E]], base=0, channel_multiplier=0, allow_small_or_imprecise_dtypes=True).then_inc(consts, 1)
            pool.iota(iota_w[:], pattern=[[1, NT]], base=0, channel_multiplier=0, allow_small_or_imprecise_dtypes=True).then_inc(consts, 1)
            pool.iota(iota_t[:], pattern=[[P, B]], base=0, channel_multiplier=1, allow_small_or_imprecise_dtypes=True).then_inc(consts, 1)
            pool.iota(iota_p[:], pattern=[[0, 1]], base=0, channel_multiplier=1, allow_small_or_imprecise_dtypes=True).then_inc(consts, 1)
            pool.iota(low6[:], pattern=[[0, 1]], base=-1, channel_multiplier=K, allow_small_or_imprecise_dtypes=True).then_inc(consts, 1)
            pool.iota(c128[:], pattern=[[P, 7]], base=P, channel_multiplier=0, allow_small_or_imprecise_dtypes=True).then_inc(consts, 1)
            pool.iota(iota_q[:], pattern=[[1, NOV]], base=0, channel_multiplier=0, allow_small_or_imprecise_dtypes=True).then_inc(consts, 1)
            pool.wait_ge(consts, 8)
            pool.sem_inc(consts, 1)

            pool.wait_ge(var_done, 1)
            pool.tensor_tensor(rstd[:, :], var[:, :], neg_half[:, :], ALU.pow).then_inc(rstd_done, 1)

            for j in range(B):
                pool.wait_ge(highs, j + 1)
                if j >= 2:
                    m = j - 2
                    pool.wait_ge(parts_out[m % (B // 2)], 32 * (m // (B // 2) + 1))
                pool.tensor_tensor(low[:, j % 2, :], full[:, j % 2, :], high[:, j % 2, :].bitcast(F32), ALU.subtract).then_inc(lows, 1)

            pool.wait_ge(taken, 4)
            pool.wait_ge(mask_col, 1)
            for b in range(B):
                if b >= 2:
                    pool.wait_ge(pv_done, 4 * (b - 1))
                for s in range(TC):
                    last = pool.tensor_scalar(v_pad[:, b % 2, s, :, 0:D],
                                              vals[:, b * TC + s, :].rearrange("p (h d) -> p h d", d=D),
                                              mask_c[:, b * TC + s:b * TC + s + 1], None, ALU.mult)
                last.then_inc(v_ready, 1)

            pool.wait_ge(var_done, 2)
            pool.tensor_tensor(rstd[:, :], var[:, :], neg_half[:, :], ALU.pow).then_inc(rstd_done, 1)
            pool.wait_ge(tok_out, 16 * B)

            def gather(e):
                pool.wait_ge(idx, e.v + 1)
                if not first(e, 4):
                    pool.wait_ge(xpose, e.v - 3)
                pool.sem_inc(pool_steps, 1)
                pool.indirect_dma_start(
                    out=rows[:, e.r % 4, :], out_offset=None, in_=tokens,
                    in_offset=bass.IndirectOffsetOnAxis(ap=g_idx[:, e.r:e.r + 1], axis=0)).then_inc(rows_in[e.r % 4], 16)

            def scatter(e):
                pool.wait_ge(y_done, e.v + 1)
                pool.sem_inc(pool_steps, 1)
                pool.indirect_dma_start(
                    out=routed, out_offset=bass.IndirectOffsetOnAxis(ap=s_idx[:, e.r:e.r + 1], axis=0),
                    in_=y_sb[:, e.r % 4, :], in_offset=None, bounds_check=NT * K - 1,
                    oob_is_err=False).then_inc(y_out[e.r % 4], 16)

            experts(pool, [(0, scatter), (L_GATHER, gather)])
            pool.wait_ge(plan_done, 1)
            n_over = pool.value_load(plan[0:1, 2 * NOV:2 * NOV + 1], min_val=0, max_val=NOV)
            for r in range(4):
                pool.wait_ge(y_out[r], 16 * E // 4)
            pool.sem_inc(v_free, 1)
            with pool.If(n_over > 0):
                with pool.Fori(0, n_over) as i:
                    pool.wait_ge(v_idx, i + 1)
                    pool.sem_inc(pool_steps, 1)
                    pool.indirect_dma_start(
                        out=rows[:, 0, :], out_offset=None, in_=tokens,
                        in_offset=bass.IndirectOffsetOnAxis(ap=g_idx[:, 0:1], axis=0)).then_inc(v_rows, 16)
                    pool.wait_ge(v_y, i + 1)
                    pool.sem_inc(pool_steps, 1)
                    pool.indirect_dma_start(
                        out=routed, out_offset=bass.IndirectOffsetOnAxis(ap=s_idx[:, 0:1], axis=0),
                        in_=y_sb[:, 0, :], in_offset=None, bounds_check=NT * K - 1,
                        oob_is_err=False).then_inc(v_out, 16)
                    pool.wait_ge(v_out, 16 * i + 16)
                    pool.sem_inc(v_free, 1)
            with pool.Else():
                pool.nop()
            pool.sem_inc(scattered, 1)

        @block.scalar
        def _(act):
            n = [0]
            act.dma_start(mask_r[:, :], mask.rearrange("b (s p) -> (b s) p", p=P)).then_inc(ld_mask, 16)
            act.dma_start(mask_b[:, :], mask).then_inc(ld_mask, 16)
            act.dma_start(b_sb[:, 0:1], bk).then_inc(ld_small, 16)
            act.dma_start(b_sb[:, 1:2], bq).then_inc(ld_small, 16)
            act.dma_start(bv_sb[:, :], bv.to_broadcast([P, P])).then_inc(ld_small, 16)
            act.dma_start(g_sb[:, 0:1], g_xattn.to_broadcast([P, 1])).then_inc(ld_small, 16)
            act.dma_start(g_sb[:, 1:2], g_ffn.to_broadcast([P, 1])).then_inc(ld_small, 16)
            act.wait_ge(zero_col, 1)
            for n in range(1, 3):
                for st in (q_st[n], k_st[n]):
                    last = act.activation(st[0:AROWS, :, :].rearrange("p h t -> p (h t)"),
                                          zeros[0:AROWS, :].to_broadcast([AROWS, H * T]), ACT.Copy)
            last.then_inc(zeroed, 1)
            act.wait_ge(ld_small, 80)
            act.activation(tg[:, 0:2], g_sb[:, :], ACT.Tanh).then_inc(tanh_g, 1)
            for j in range(B):
                act.wait_ge(fulls, j + 1)
                if j >= 2:
                    half = j - 2
                    act.wait_ge(parts_out[half % (B // 2)], 32 * (half // (B // 2) + 1))
                act.activation(high[:, j % 2, :], full[:, j % 2, :], ACT.Copy).then_inc(highs, 1)

            for a in range(STEPS + 2):
                p = pair_of(a)
                if p is not None:
                    act.wait_ge(b_done, p + 1)
                    if p >= 4:
                        act.wait_ge(pv_done, (p - 4) // 2 + 1)
                    act.activation(probs[:, p % 4, 0:1024], score[p % 2][:, :], ACT.Exp, scale=1.0 / ROOT).then_inc(exp_done, 1)
                gq = group_of(a - 1)
                if gq is not None:
                    b, g = divmod(gq, 4)
                    act.wait_ge(pv_done, gq + 1)
                    if b >= 2 and g == 0:
                        act.wait_ge(x1_done, b - 1)
                    act.activation(o_sb[:, b % 2, g, :], bank[6][:, 0:T], ACT.Copy).then_inc(os_done, 1)

            for b in range(B):
                act.wait_ge(xt_ready, b + 1)
                act.activation(xt[:, :, b * P:(b + 1) * P], bank[b % 2][:, 0:TC * P].rearrange("p (k n) -> p k n", k=TC),
                               ACT.Copy).then_inc(xt_done, 1)
            act.wait_ge(lg_ready, 1)
            act.activation(logits[:, :, :], bank[2][:, 0:B * E].rearrange("p (b e) -> p b e", b=B), ACT.Copy).then_inc(lg_done, 1)
            act.wait_ge(soft, 1)
            act.activation(e6[:, :, :], e6[:, :, :], ACT.Exp).then_inc(softd, 1)
            for j in range(8):
                act.wait_ge(sg_ready, j + 1)
                if j >= 2:
                    act.wait_ge(sh_done, j - 1)
                act.activation(s_th[:, j % 2, :], bank[3 + 2 * (j % 2)][0:IC, :], ACT.Tanh, scale=0.5).then_inc(sth_done, 1)

            def pick(e):
                if not first(e, 4):
                    act.wait_ge(inv, e.v - 3)
                act.activation(picked[:, e.r % 4, :, :], route[:, :, bass.ds(e.v, 1), :].rearrange("p b o n -> p b (o n)"),
                               ACT.Copy).then_inc(pick_done, 1)

            def take_x(e):
                act.wait_ge(xpose, e.v + 1)
                if not first(e, 2):
                    act.wait_ge(s1, e.v - 1)
                act.activation(xe[:, e.r % 2, :, :], bank[1 + e.r % 2][:, 0:TC * P].rearrange("p (k n) -> p k n", k=TC),
                               ACT.Copy).then_inc(xe_done, 1)

            def tanh(e):
                act.wait_ge(s1, e.v + 1)
                if not first(e, 2):
                    act.wait_ge(hs_done, e.v - 1)
                act.activation(th[:, e.r % 2, :], bank[3 + e.r % 2][0:IC, 0:2 * P], ACT.Tanh, scale=0.5).then_inc(th_done, 1)

            def take_y(e):
                act.wait_ge(s2, e.v + 1)
                if not first(e, 4):
                    act.wait_ge(y_out[e.r % 4], 16 * e.use(4))
                act.activation(y_sb[:, e.r % 4, :], bank[5 + e.r % 2][:, 0:T], ACT.Copy).then_inc(y_done, 1)

            act.wait_ge(route_done, 1)
            experts(act, [(L_PICK, pick), (0, take_y), (L_S1, tanh), (L_X, take_x)])
            act.wait_ge(plan_done, 1)
            n_over = act.value_load(plan[0:1, 2 * NOV:2 * NOV + 1], min_val=0, max_val=NOV)
            for r in range(4):
                act.wait_ge(y_out[r], 16 * E // 4)
            with act.If(n_over > 0):
                with act.Fori(0, n_over) as i:
                    e = act.value_load(plan[0:1, bass.ds(i, 1)], min_val=0, max_val=E - 1)
                    act.activation(picked[:, 0, :, :], route[:, :, bass.ds(e, 1), :].rearrange("p b o n -> p b (o n)"),
                                   ACT.Copy).then_inc(v_pick, 1)
                    act.wait_ge(v_x, i + 1)
                    act.activation(xe[:, 0, :, :], bank[1][:, 0:TC * P].rearrange("p (k n) -> p k n", k=TC),
                                   ACT.Copy).then_inc(v_xe, 1)
                    act.wait_ge(v_s1, i + 1)
                    act.activation(th[:, 0, :], bank[3][0:IC, 0:2 * P], ACT.Tanh, scale=0.5).then_inc(v_th, 1)
                    act.wait_ge(v_s2, i + 2)
                    act.wait_ge(v_free, i + 1)
                    act.activation(y_sb[:, 0, :], bank[5][:, 0:T], ACT.Copy).then_inc(v_y, 1)
            with act.Else():
                act.nop()

        @block.vector
        def _(dve):
            n = [0]

            def link(ins):
                n[0] += 1
                ins.then_inc(dv, 1)
                dve.wait_ge(dv, n[0])

            dve.memset(q_st[0][0:AROWS, :, :].bitcast(F32), 0.0)
            dve.memset(k_st[0][0:AROWS, :, :].bitcast(F32), 0.0).then_inc(zeroed, 1)
            dve.wait_ge(ld_mask, 32)
            link(dve.tensor_scalar(mask_k[:, :], mask_b[:, :], NEG * ROOT, -NEG * ROOT, ALU.mult, ALU.add))
            for m, src in enumerate((mask_b, mask_k)):
                dve.tensor_copy(mask_hl[:, 2 * m, :], src[:, :]).then_inc(aug, 1)
                dve.wait_ge(aug, 2 * m + 1)
                dve.tensor_tensor(mask_hl[:, 2 * m + 1, :], src[:, :], mask_hl[:, 2 * m, :].bitcast(F32), ALU.subtract).then_inc(aug, 1)
            dve.wait_ge(proj, 1)
            dve.tensor_copy(mask_c[:, :], bank[0][:, 0:B * TC]).then_inc(mask_col, 1)

            def variances():
                for b in range(B):
                    last = dve.bn_stats(stats[:, b, :], x_sb[:, b, :])
                link(last)
                for b in range(B):
                    last = dve.bn_aggr(mv[:, b, :], stats[:, b, :])
                link(last)
                dve.tensor_scalar(var[:, :], mv[:, :, 1], EPS, None, ALU.add).then_inc(var_done, 1)

            def normalize(bs, done):
                for b in bs:
                    dve.tensor_scalar(xn[:, b, :], x_sb[:, b, :], mv[:, b, 0:1], rstd[:, b:b + 1],
                                      ALU.subtract, ALU.mult).then_inc(done, 1)

            dve.wait_ge(ld_x, 16)
            variances()
            dve.wait_ge(ld_small, 80)
            dve.wait_ge(ld_bc, 16)
            for j in range(B):
                if j == 1:
                    dve.wait_ge(rstd_done, 1)
                    normalize(range(B), normed)
                dve.wait_ge(proj, j + 2)
                if j >= 2:
                    dve.wait_ge(lows, j - 1)
                c = (j % (B // 2)) * 2 * T
                dve.scalar_tensor_tensor(full[:, j % 2, :], bank[(j + 1) % 8], b_sb[:, j // (B // 2):j // (B // 2) + 1],
                                         mask_bc[:, c:c + 2 * T], ALU.add, ALU.mult).then_inc(fulls, 1)
            for j in range(4):
                dve.wait_ge(proj, 10 + j)
                dve.tensor_tensor(vals[:, 4 * j:4 * j + 4, :], bank[(j + 1) % 8].rearrange("p (s n) -> p s n", s=4),
                                  bv_sb[:, :].rearrange("p (o n) -> p o n", o=1).to_broadcast([P, 4, P]), ALU.add).then_inc(taken, 1)
            dve.wait_ge(tanh_g, 1)
            dve.wait_ge(mask_col, 1)

            t_seen = 0
            for a in range(STEPS + 2):
                if a < NA:
                    dve.wait_ge(a_done, a + 1)
                    b, h = divmod(a, H)
                    if b >= 2 and h == 0:
                        dve.wait_ge(t_ready, t_index[("max", b - 2, 0)] + 1)
                    dve.tensor_reduce(mx[:, b % 2, :, h], bank[a % 2].rearrange("p (c s) -> p c s", c=TC),
                                      AX.X, ALU.max).then_inc(max_done, 1)
                for kind, b, c in events.get(a - 1, []):
                    t_seen += 1
                    dve.wait_ge(t_ready, t_seen)
                    if kind == "max":
                        if b >= 2:
                            dve.wait_ge(max_out, 32 * (b - 1))
                        src = bank[7][0:H, 0:T]
                        dve.tensor_scalar(nm[:, b % 2, 0, :], src, -1.0, None, ALU.mult).then_inc(nm_done, 1)
                        dve.wait_ge(nm_done, 2 * b + 1)
                        dve.scalar_tensor_tensor(nm[:, b % 2, 1, :], src, -1.0, nm[:, b % 2, 0, :].bitcast(F32),
                                                 ALU.mult, ALU.subtract).then_inc(nm_done, 1)
                    elif kind == "out":
                        src = bank[7].rearrange("p (h r) -> p h r", r=32)
                        link(dve.reciprocal(rz[:, 0, :], src[:, :, D]))
                        link(dve.tensor_scalar(rz[:, 1, :], rz[:, 0, :], mask_c[:, b * TC + c:b * TC + c + 1], None, ALU.mult))
                        dve.tensor_tensor(o_n[:, c, :].rearrange("p (h d) -> p h d", d=D), src[:, :, 0:D],
                                          rz[:, 1, :].rearrange("p (h o) -> p h o", o=1).to_broadcast([P, H, D]),
                                          ALU.mult).then_inc(on_done, 1)
                    else:
                        dve.scalar_tensor_tensor(x_sb[:, b, :], bank[7][:, 0:T], tg[:, 0:1], x_sb[:, b, :],
                                                 ALU.mult, ALU.add).then_inc(x1_done, 1)

            dve.wait_ge(x1_done, B)
            variances()
            dve.wait_ge(rstd_done, 2)
            normalize(range(B), tok_normed)
            dve.tensor_scalar(tg[:, 2:3], tg[:, 1:2], 0.5, None, ALU.mult)
            dve.wait_ge(lg_done, 1)
            for b in range(B):
                last = dve.max(v8[:, b, :], logits[:, b, :])
            link(last)
            for b in range(B):
                last = dve.max_index(i8[:, b, :], v8[:, b, :], logits[:, b, :])
            link(last)
            dve.tensor_tensor(e6[:, :, :], v8[:, :, 0:K], v8[:, :, 0:1].to_broadcast([P, B, K]), ALU.subtract).then_inc(soft, 1)
            link(dve.tensor_copy(if8[:, :, :], i8[:, :, :]))
            dve.wait_ge(consts, 9)
            for k in range(K):
                dst = rank if k == 0 else eq
                link(dve.tensor_tensor(dst[:, :, :], iota_e[:, :].rearrange("p (o e) -> p o e", o=1).to_broadcast([P, B, E]),
                                       if8[:, :, k:k + 1].to_broadcast([P, B, E]), ALU.is_equal))
                if k:
                    link(dve.scalar_tensor_tensor(rank[:, :, :], eq[:, :, :], float(k + 1), rank[:, :, :], ALU.mult, ALU.add))
            dve.tensor_scalar(chosen[:, :, :], rank[:, :, :], 1.0, None, ALU.min).then_inc(chosen_done, 1)
            dve.tensor_scalar(far[:, :, :], rank[:, :, :], 1.0, None, ALU.min)
            for b in range(B):
                dve.memset(route[:, b, :, 2], float(K * P * b - FAR))
                dve.tensor_scalar(route[:, b, :, 1], iota_e[:, :], 0.0, iota_t[:, b:b + 1], ALU.mult, ALU.add)
            link(dve.tensor_scalar(route[:, :, :, 3], rank[:, :, :], low6[:, 0:1], None, ALU.add))
            link(dve.tensor_scalar(far[:, :, :], far[:, :, :], float(FAR), -float(FAR), ALU.mult, ALU.add))
            dve.wait_ge(pos_ready, 1)
            dve.tensor_tensor(route[:, :, :, 0], bank[7].rearrange("p (b e) -> p b e", b=B), far[:, :, :], ALU.add).then_inc(route_done, 1)
            dve.wait_ge(softd, 1)
            link(dve.tensor_reduce(e6s[:, :], e6[:, :, :], AX.X, ALU.add))
            link(dve.reciprocal(e6s[:, :], e6s[:, :]))
            link(dve.tensor_scalar(e6s[:, :], e6s[:, :], tg[:, 2:3], None, ALU.mult))
            dve.tensor_tensor(ww[:, :, :], e6[:, :, :], e6s[:, :].rearrange("p (b o) -> p b o", o=1).to_broadcast([P, B, K]), ALU.mult)
            dve.wait_ge(cnt_ready, 1)
            link(dve.tensor_copy(n_e[:, :], bank[6][0:E, 0:1]))
            link(dve.tensor_scalar(c_tmp[:, :], c128[:, :], n_e[:, 0:1], None, ALU.is_lt))
            dve.tensor_reduce(extra[:, :], c_tmp[:, :], AX.X, ALU.add).then_inc(beg_in, 1)
            dve.wait_ge(beg_ready, 1)
            link(dve.tensor_copy(o_beg[:, :], bank[6][0:E, 8:9]))
            link(dve.tensor_tensor(o_end[:, :], o_beg[:, :], extra[:, :], ALU.add))
            link(dve.tensor_scalar(t_ge[:, :], iota_q[:, :], o_beg[:, 0:1], None, ALU.is_ge))
            link(dve.scalar_tensor_tensor(t_in[:, :], iota_q[:, :], o_end[:, 0:1], t_ge[:, :], ALU.is_lt, ALU.mult))
            link(dve.tensor_scalar(t_c[:, :], iota_q[:, :], o_beg[:, 0:1], 1.0, ALU.subtract, ALU.add))
            dve.tensor_tensor(t_c2[:, :], t_c[:, :], t_in[:, :], ALU.mult).then_inc(plan_in, 1)
            dve.wait_ge(plan_ready, 1)
            dve.tensor_copy(plan[0:1, :], bank[6][0:1, 16:16 + 2 * NOV + 1]).then_inc(plan_done, 1)

            for j in range(8):
                g_ps, u_ps = bank[3 + 2 * (j % 2)][0:IC, :], bank[3 + 2 * (j % 2) + 1][0:IC, :]
                nb, c = divmod(j, 4)
                dve.wait_ge(sth_done, j + 1)
                link(dve.scalar_tensor_tensor(s_gg[:, j % 2, :], s_th[:, j % 2, :], 1.0, g_ps, ALU.add, ALU.mult))
                dve.tensor_tensor(s_h[:, c, nb * 512:(nb + 1) * 512], s_gg[:, j % 2, :], u_ps, ALU.mult).then_inc(sh_done, 1)
            for b in range(B):
                dve.wait_ge(sdn_ready, b + 1)
                dve.scalar_tensor_tensor(x_sb[:, b, :], bank[1 + b % 2][:, 0:T], tg[:, 2:3], x_sb[:, b, :],
                                         ALU.mult, ALU.add).then_inc(acc_done, 1)

            def hot_rows(e):
                dve.wait_ge(pick_done, e.v + 1)
                if not first(e, 2):
                    dve.wait_ge(inv, e.v - 1)
                dve.tensor_tensor(onehot[:, e.r % 2, :, :],
                                  iota_w[:, 0:P].rearrange("p (o j) -> p o j", o=1).to_broadcast([P, B, P]),
                                  picked[:, e.r % 4, :, 0:1].to_broadcast([P, B, P]), ALU.is_equal).then_inc(hot, 1)

            def indices(e):
                dve.wait_ge(inv, e.v + 1)
                if not first(e, 8):
                    dve.wait_ge(y_out[e.r % 4], 16 * (e.use(4) - 1))
                src = bank[7 * (e.r % 2)][:, 0:3]
                dve.tensor_copy(g_idx[:, e.r:e.r + 1], src[:, 0:1])
                dve.tensor_scalar(s_idx[:, e.r:e.r + 1], src[:, 1:2], float(FAR), src[:, 2:3],
                                  ALU.add, ALU.add).then_inc(idx, 1)

            def hidden(e):
                dve.wait_ge(th_done, e.v + 1)
                if not first(e, 2):
                    dve.wait_ge(s2, e.v - 1)
                dve.scalar_tensor_tensor(hs[:, e.r % 2, :, :].rearrange("p c n -> p (c n)"), th[:, e.r % 2, :], 1.0,
                                         bank[3 + e.r % 2][0:IC, 0:2 * P], ALU.add, ALU.mult).then_inc(hs_done, 1)

            dve.wait_ge(route_done, 1)
            experts(dve, [(L_HOT, hot_rows), (L_IDX, indices), (L_S1, hidden)])
            dve.wait_ge(plan_done, 1)
            n_over = dve.value_load(plan[0:1, 2 * NOV:2 * NOV + 1], min_val=0, max_val=NOV)
            for r in range(4):
                dve.wait_ge(y_out[r], 16 * E // 4)
            with dve.If(n_over > 0):
                with dve.Fori(0, n_over) as i:
                    c = dve.value_load(plan[0:1, bass.ds(i + NOV, 1)], min_val=1, max_val=7)
                    dve.wait_ge(v_pick, i + 1)
                    dve.tensor_tensor(onehot[:, 0, :, :],
                                      iota_w[:, bass.ds(c * P, P)].rearrange("p (o j) -> p o j", o=1).to_broadcast([P, B, P]),
                                      picked[:, 0, :, 0:1].to_broadcast([P, B, P]), ALU.is_equal).then_inc(v_hot, 1)
                    dve.wait_ge(v_inv, i + 1)
                    dve.wait_ge(v_free, i + 1)
                    src = bank[0][:, 0:3]
                    dve.tensor_copy(g_idx[:, 0:1], src[:, 0:1])
                    dve.tensor_scalar(s_idx[:, 0:1], src[:, 1:2], float(FAR), src[:, 2:3],
                                      ALU.add, ALU.add).then_inc(v_idx, 1)
                    dve.wait_ge(v_th, i + 1)
                    dve.scalar_tensor_tensor(hs[:, 0, :, :].rearrange("p c n -> p (c n)"), th[:, 0, :], 1.0,
                                             bank[3][0:IC, 0:2 * P], ALU.add, ALU.mult).then_inc(v_hs, 1)
            with dve.Else():
                dve.nop()
            for b in range(B):
                dve.wait_ge(y6_in[b % 2], 16 * (b // 2 + 1))
                for k in range(K):
                    ins = dve.scalar_tensor_tensor(x_sb[:, b, :], y6[:, b % 2, k, :], ww[:, b, k:k + 1], x_sb[:, b, :],
                                                   ALU.mult, ALU.add)
                    if k < K - 1:
                        link(ins)
                ins.then_inc(mixed, 1)

        @block.tensor
        def _(pe):
            mm = nc.tensor.matmul
            tr = nc.tensor.transpose

            def t_taken(kind, b, c):
                return {"max": (nm_done, 2 * (b + 1)), "out": (on_done, 2 * b + c + 1), "back": (x1_done, b + 1)}[kind]

            pe.wait_ge(consts, 9)
            pe.wait_ge(ld_mask, 32)
            tr(bank[0][:, 0:B * TC], mask_r[:, :], ident[0:B * TC, 0:B * TC]).then_inc(proj, 1)
            pe.wait_ge(ld_ctx, 16)
            pe.wait_ge(ld_w, 48)
            for j in range(B):
                k_side, c = j < B // 2, 2 * (j % (B // 2))
                if not k_side:
                    pe.wait_ge(normed, c + 2)
                if j == 7:
                    pe.wait_ge(mask_col, 1)
                src = (ctx_sb if k_side else xn)[:, c:c + 2, :].rearrange("p b t -> p (b t)")
                mm(bank[(j + 1) % 8], w_sb[:, 0 if k_side else 1, :], src, start=True, stop=True).then_inc(proj, 1)
            for j in range(4):
                pe.wait_ge(fulls, j + 1)
                for s in range(4):
                    b, c = divmod(4 * j + s, TC)
                    last = mm(bank[(j + 1) % 8][:, s * P:(s + 1) * P], ctx_sb[:, b, c * P:(c + 1) * P], w_sb[:, 2, :],
                              start=True, stop=True)
                last.then_inc(proj, 1)
            pe.wait_ge(fulls, B)
            pe.wait_ge(taken, 4)

            t_last = None
            for a in range(STEPS):
                if a < NA:
                    b, h = divmod(a, H)
                    if h == 0:
                        pe.wait_ge(stack_in[b % 3], 80 * (b // 3 + 1))
                    if a >= 2:
                        pe.wait_ge(max_done, a - 1)
                    for c in range(TC):
                        last = mm(bank[a % 2][:, c * T:(c + 1) * T], q_st[b % 3][0:AROWS, h, c * P:(c + 1) * P],
                                  k_st[b % 3][0:AROWS, h, :], start=True, stop=True)
                    last.then_inc(a_done, 1)
                p = pair_of(a)
                if p is not None:
                    b, h = divmod(2 * p, H)
                    if h == 0:
                        pe.wait_ge(max_in, 16 * (b + 1))
                        pe.wait_ge(ones_in, 48)
                    if p >= 2:
                        pe.wait_ge(exp_done, p - 1)
                    for i in range(2):
                        for c in range(TC):
                            o = (i * TC + c) * T
                            last = mm(score[p % 2][:, o:o + T], k_st[b % 3][0:BROWS, h + i, c * P:(c + 1) * P],
                                      q_st[b % 3][0:BROWS, h + i, :], start=True, stop=True)
                    last.then_inc(b_done, 1)
                gq = group_of(a)
                if gq is not None:
                    b, g = divmod(gq, 4)
                    pe.wait_ge(exp_done, 2 * gq + 2)
                    if gq >= 1:
                        pe.wait_ge(os_done, gq)
                    if g == 0:
                        pe.wait_ge(v_ready, b + 1)
                    for c in range(TC):
                        for i in range(4):
                            pr = probs[:, (2 * gq + i // 2) % 4, :].rearrange("p (i c t) -> p i c t", i=2, c=TC)
                            last = mm(bank[6][32 * i:32 * i + 32, 0:T], v_pad[:, b % 2, c, 4 * g + i, :],
                                      pr[:, i % 2, c, :], start=(c == 0), stop=(c == TC - 1))
                    last.then_inc(pv_done, 1)
                for kind, b, c in events.get(a, []):
                    if t_last is not None:
                        pe.wait_ge(*t_taken(*t_last))
                    t_last = (kind, b, c)
                    if kind == "max":
                        pe.wait_ge(max_done, 16 * (b + 1))
                        for i in range(TC):
                            last = tr(bank[7][0:H, i * P:(i + 1) * P], mx[:, b % 2, i, :], ident[:, :])
                    elif kind == "out":
                        pe.wait_ge(os_done, 4 * (b + 1))
                        for g in range(4):
                            last = tr(bank[7][:, g * P:(g + 1) * P], o_sb[:, b % 2, g, c * P:(c + 1) * P], ident[:, :])
                    else:
                        pe.wait_ge(on_done, 2 * (b + 1))
                        for i in range(TC):
                            last = tr(bank[7][:, i * P:(i + 1) * P], o_n[:, i, :], ident[:, :])
                    last.then_inc(t_ready, 1)

            for b in range(B):
                pe.wait_ge(tok_normed, b + 1)
                if b >= 2:
                    pe.wait_ge(xt_done, b - 1)
                for k in range(TC):
                    last = tr(bank[b % 2][:, k * P:(k + 1) * P], xn[:, b, k * P:(k + 1) * P], ident[:, :])
                last.then_inc(xt_ready, 1)
            pe.wait_ge(ld_gate, 16)
            pe.wait_ge(exp_done, NP)
            for b in range(B):
                pe.wait_ge(xt_done, b + 1)
                for k in range(TC):
                    last = mm(bank[2][:, b * E:(b + 1) * E], xt[:, k, b * P:(b + 1) * P], gate_sb[:, k, :],
                              start=(k == 0), stop=(k == TC - 1))
            last.then_inc(lg_ready, 1)

            def shared_up(j):
                nb, c = divmod(j, 4)
                if j >= 2:
                    pe.wait_ge(sh_done, j - 1)
                for half in range(2):
                    for k in range(TC):
                        last = mm(bank[3 + 2 * (j % 2) + half][0:IC, :], sgu_sb[:, k, 4 * half + c, :],
                                  xt[:, k, nb * 512:(nb + 1) * 512], start=(k == 0), stop=(k == TC - 1))
                last.then_inc(sg_ready, 1)

            pe.wait_ge(x1_done, B)
            pe.wait_ge(chosen_done, 1)
            for b in range(B):
                for b2 in range(b + 1):
                    last = mm(bank[7][:, b * E:(b + 1) * E], (tri if b2 == b else ones16)[:, :], chosen[:, b2, :],
                              start=(b2 == 0), stop=(b2 == b))
            last.then_inc(pos_ready, 1)
            pe.wait_ge(os_done, NG)
            for b in range(B):
                last = mm(bank[6][0:E, 0:1], chosen[:, b, :], ones16[:, 0:1], start=(b == 0), stop=(b == B - 1))
            last.then_inc(cnt_ready, 1)
            pe.wait_ge(beg_in, 1)
            mm(bank[6][0:E, 8:9], tri_f[:, :], extra[:, :], start=True, stop=True).then_inc(beg_ready, 1)
            pe.wait_ge(plan_in, 1)
            mm(bank[6][0:1, 16:16 + NOV], iota_p[0:E, :], t_in[:, :], start=True, stop=True)
            mm(bank[6][0:1, 16 + NOV:16 + 2 * NOV], ones_f[:, :], t_c2[:, :], start=True, stop=True)
            mm(bank[6][0:1, 16 + 2 * NOV:17 + 2 * NOV], ones_f[:, :], extra[:, :], start=True, stop=True).then_inc(plan_ready, 1)
            pe.wait_ge(plan_done, 1)
            pe.wait_ge(ld_shared, 32)
            for j in range(8):
                shared_up(j)
            pe.wait_ge(lg_done, 1)
            for b in range(B):
                pe.wait_ge(sh_done, 4 * (b // 4 + 1))
                if b >= 2:
                    pe.wait_ge(acc_done, b - 1)
                for c in range(4):
                    last = mm(bank[1 + b % 2][:, 0:T], s_h[:, c, b * P:(b + 1) * P], sd_sb[:, c, :],
                              start=(c == 0), stop=(c == 3))
                last.then_inc(sdn_ready, 1)
            pe.wait_ge(acc_done, B)

            def invert(e):
                pe.wait_ge(hot, e.v + 1)
                if not first(e, 2):
                    pe.wait_ge(idx, e.v - 1)
                for b in range(B):
                    last = mm(bank[7 * (e.r % 2)][:, 0:3], onehot[:, e.r % 2, b, :], picked[:, e.r % 4, b, 1:4],
                              start=(b == 0), stop=(b == B - 1))
                last.then_inc(inv, 1)

            def transpose_rows(e):
                pe.wait_ge(rows_in[e.r % 4], 16 * (e.use(4) + 1))
                if not first(e, 2):
                    pe.wait_ge(xe_done, e.v - 1)
                for k in range(TC):
                    last = tr(bank[1 + e.r % 2][:, k * P:(k + 1) * P], rows[:, e.r % 4, k * P:(k + 1) * P], ident[:, :])
                last.then_inc(xpose, 1)

            def first_product(e):
                pe.wait_ge(w_in[e.r % 4], 32 * (e.use(4) + 1))
                pe.wait_ge(xe_done, e.v + 1)
                if not first(e, 2):
                    pe.wait_ge(hs_done, e.v - 1)
                for c in range(2):
                    for k in range(TC):
                        last = mm(bank[3 + e.r % 2][0:IC, c * P:(c + 1) * P], w1_sb[:, e.r % 4, k, c * IC:(c + 1) * IC],
                                  xe[:, e.r % 2, k, :], start=(k == 0), stop=(k == TC - 1))
                last.then_inc(s1, 1)

            def second_product(e):
                pe.wait_ge(hs_done, e.v + 1)
                if not first(e, 2):
                    pe.wait_ge(y_done, e.v - 1)
                for c in range(2):
                    last = mm(bank[5 + e.r % 2][:, 0:T], hs[:, e.r % 2, c, :], w2_sb[0:IC, e.r % 4, c, :],
                              start=(c == 0), stop=(c == 1))
                last.then_inc(s2, 1)

            experts(pe, [(0, second_product), (L_S1, first_product), (L_X, transpose_rows), (L_INV, invert)])
            n_over = pe.value_load(plan[0:1, 2 * NOV:2 * NOV + 1], min_val=0, max_val=NOV)
            pe.wait_ge(y_done, E)
            pe.sem_inc(v_s2, 1)
            with pe.If(n_over > 0):
                with pe.Fori(0, n_over) as i:
                    pe.wait_ge(v_hot, i + 1)
                    for b in range(B):
                        last = mm(bank[0][:, 0:3], onehot[:, 0, b, :], picked[:, 0, b, 1:4], start=(b == 0), stop=(b == B - 1))
                    last.then_inc(v_inv, 1)
                    pe.wait_ge(v_rows, 16 * i + 16)
                    for k in range(TC):
                        last = tr(bank[1][:, k * P:(k + 1) * P], rows[:, 0, k * P:(k + 1) * P], ident[:, :])
                    last.then_inc(v_x, 1)
                    pe.wait_ge(v_w, 32 * i + 32)
                    pe.wait_ge(v_xe, i + 1)
                    for c in range(2):
                        for k in range(TC):
                            last = mm(bank[3][0:IC, c * P:(c + 1) * P], w1_sb[:, 0, k, c * IC:(c + 1) * IC],
                                      xe[:, 0, k, :], start=(k == 0), stop=(k == TC - 1))
                    last.then_inc(v_s1, 1)
                    pe.wait_ge(v_hs, i + 1)
                    pe.wait_ge(v_free, i + 1)
                    for c in range(2):
                        last = mm(bank[5][:, 0:T], hs[:, 0, c, :], w2_sb[0:IC, 0, c, :], start=(c == 0), stop=(c == 1))
                    last.then_inc(v_s2, 1)
            with pe.Else():
                pe.nop()


def kernel(**inputs):
    import numpy as np
    import concourse.bacc as bacc
    from concourse.bass_utils import run_bass_kernel_spmd as run

    P, H, D, IC = 128, 16, 8, 96
    a = {k: np.asarray(v) for k, v in inputs.items()}
    by_width = np.arange(H * D).reshape(H, D).T.reshape(-1)

    def pad(w, axis, size):
        width = [(0, 0)] * w.ndim
        width[axis] = (0, size - w.shape[axis])
        return np.pad(w, width)

    E, I, T = a["L0_ffn_experts_w1"].shape
    half = I // 2
    w1 = pad(a["L0_ffn_experts_w1"].reshape(E, 2, half, T // P, P), 2, IC)
    w2 = pad(a["L0_ffn_experts_w2"].reshape(E, T, 2, half), 3, P)
    sgu = pad(a["L0_ffn_shared_gate_up"].reshape(8, half, T // P, P), 1, IC)
    sd = pad(a["L0_ffn_shared_down"].reshape(T, 4, half), 2, IC)
    laid = {
        "x": a["x"].transpose(1, 0, 2), "ctx": a["ctx_2048"].transpose(1, 0, 2), "mask": a["mask_Bx1x2048_fk1"][:, 0],
        "g_xattn": a["g_xattn"][None], "g_ffn": a["g_ffn"][None],
        "wq": a["L0_xattn_Wq"][by_width].T, "bq": a["L0_xattn_bq"][by_width][:, None],
        "wk": a["L0_xattn_Wk"][by_width].T, "bk": a["L0_xattn_bk"][by_width][:, None],
        "wv": a["L0_xattn_Wv"].T, "bv": a["L0_xattn_bv"][None],
        "gate": a["L0_ffn_gate_w"].T.reshape(T // P, P, E).transpose(1, 0, 2),
        "w1": w1.transpose(0, 4, 3, 1, 2).reshape(E, P, T // P, 2 * IC),
        "w2": w2.transpose(0, 3, 2, 1),
        "sgu": sgu.transpose(3, 2, 0, 1), "sd": sd.transpose(2, 1, 0),
    }
    nc = bacc.Bacc("TRN2", target_bir_lowering=False, num_devices=1)
    arrays, args = {}, []
    for name, w in laid.items():
        w = np.ascontiguousarray(w)
        arrays[f"in_{name}"] = w
        args.append(nc.dram_tensor(f"in_{name}", w.shape, mybir.dt.from_np(w.dtype), kind="ExternalInput").ap())
    out = nc.dram_tensor("out", (P, a["x"].shape[0], T), mybir.dt.float32, kind="ExternalOutput").ap()
    build_gated_block(nc, *args, out)
    r = run(nc, [arrays], core_ids=[0])
    return np.ascontiguousarray(np.asarray(r.results[0]["out"]).transpose(1, 0, 2))
```

```python
import concourse.bass as bass
from concourse import mybir
from contextlib import ExitStack


def build_gated_block(nc, x, ctx_in, mask, g_xattn, g_ffn, wq, bq, wk, bk, wv, bv, gate, w1, w2, sgu, sd, out):
    F32, F32R, F16, U32, I32 = (mybir.dt.float32, mybir.dt.float32r, mybir.dt.float16, mybir.dt.uint32,
                                mybir.dt.int32)
    ALU, ACT, AX = mybir.AluOpType, mybir.ActivationFunctionType, mybir.AxisListType

    P = 128
    B, T = x.shape[1], x.shape[2]
    H, D = 16, 8
    TC = T // P
    E = gate.shape[2]
    K = 6
    OVER = 2
    TILES = E + OVER
    NT = B * P
    IC = sd.shape[0]
    EPS = 1e-5
    NEG = 1000000.0
    ROOT = float(D) ** 0.5
    HD1 = D + 1
    PART = 2 * HD1
    SROWS = 2 * PART
    AROWS = 96
    BROWS = AROWS + 2
    FAR = 8192

    es = ExitStack()
    with es:
        def sb(name, shape, dt=F32):
            return es.enter_context(nc.sbuf_tensor(name, shape, dt))

        def sem(name):
            return es.enter_context(nc.semaphore(name))

        q_parts = nc.dram_tensor("q_parts", [B, 2, HD1 * H, T], F32).ap()
        k_parts = nc.dram_tensor("k_parts", [B, 2, HD1 * H, T], F32).ap()
        max_parts = nc.dram_tensor("max_parts", [B, 2, H, T], F32).ap()
        tokens = nc.dram_tensor("tokens", [NT, T], F32).ap()
        routed = nc.dram_tensor("routed", [NT * K, T], F32).ap()

        x_sb = sb("x_sb", [P, B, T])
        ctx_sb = sb("ctx_sb", [P, B, T])
        xn = sb("xn", [P, B, T])
        vals = sb("vals", [P, B * TC, P])
        v_pad = sb("v_pad", [P, 2, TC, H, 32])
        probs = sb("probs", [P, 4, 2 * TC * T])
        o_sb = sb("o_sb", [P, 2, 4, T])
        o_n = sb("o_n", [P, TC, P])
        full = sb("full", [P, 2, 2 * T])
        high = sb("high", [P, 2, 2 * T], F32R)
        low = sb("low", [P, 2, 2 * T], F32R)
        w_sb = sb("w_sb", [P, 3, P])
        b_sb = sb("b_sb", [P, 2])
        bv_sb = sb("bv_sb", [P, P])
        mask_bc = sb("mask_bc", [P, B * T])
        mask_r = sb("mask_r", [B * TC, P])
        mask_c = sb("mask_c", [P, B * TC])
        mask_b = sb("mask_b", [B, T])
        mask_k = sb("mask_k", [B, T])
        mask_hl = sb("mask_hl", [B, 4, T], F32R)
        ident = sb("ident", [P, P])
        zeros = sb("zeros", [P, 1])
        ones_st = sb("ones_st", [2, T])
        stats = sb("stats", [P, B, 6])
        mv = sb("mv", [P, B, 2])
        var = sb("var", [P, B])
        rstd = sb("rstd", [P, B])
        neg_half = sb("neg_half", [P, B])
        mx = sb("mx", [P, 2, TC, H])
        nm = sb("nm", [H, 2, 2, T], F32R)
        rz = sb("rz", [P, 2, H])
        g_sb = sb("g_sb", [P, 2])
        tg = sb("tg", [P, 3])
        xt = ctx_sb[:, :, :].rearrange("p b t -> p (b t)").rearrange("p (k n) -> p k n", k=TC)
        gate_sb = sb("gate_sb", [P, TC, E])
        v8 = sb("v8", [P, B, 8])
        i8 = sb("i8", [P, B, 8], U32)
        if8 = sb("if8", [P, B, 8])
        iota_e = sb("iota_e", [P, E])
        route = vals[:, :, :].rearrange("p s n -> p (s n)").bitcast(F16)[:, 0:B * E * 4].rearrange("p (b e n) -> p b e n", b=B, e=E)
        picked = sb("picked", [P, 4, B, 4], F16)
        iota_w = sb("iota_w", [P, NT + P], F16)
        iota_t = sb("iota_t", [P, B])
        iota_p = sb("iota_p", [P, 1])
        low6 = sb("low6", [P, 1])
        tri = sb("tri", [P, P], F16)
        tri_f = sb("tri_f", [E, E])
        ones16 = sb("ones16", [P, P], F16)
        ones_f = sb("ones_f", [E, 1])
        e6 = sb("e6", [P, B, K])
        e6s = sb("e6s", [P, B])
        ww = sb("ww", [P, B, K])
        n_e = sb("n_e", [E, 1])
        c128 = sb("c128", [E, 7])
        c_tmp = sb("c_tmp", [E, 7])
        extra = sb("extra", [E, 1])
        o_beg = sb("o_beg", [E, 1])
        o_end = sb("o_end", [E, 1])
        NOV = NT * K // (P + 1)
        iota_q = sb("iota_q", [E, NOV])
        t_ge = sb("t_ge", [E, NOV])
        t_in = sb("t_in", [E, NOV])
        t_c = sb("t_c", [E, NOV])
        t_c2 = sb("t_c2", [E, NOV])
        plan = sb("plan", [1, 2 * NOV + 1], I32)

        g_idx = sb("g_idx", [P, 8], U32)
        s_idx = sb("s_idx", [P, 8], U32)

        with ExitStack() as attention:
            q_st, k_st = ([attention.enter_context(nc.sbuf_tensor(f"{name}{n}", [P, H, T], F32R)) for n in range(3)]
                          for name in ("q_st", "k_st"))
        sgu_sb = sb("sgu_sb", [P, TC, 8, IC])
        sd_sb = sb("sd_sb", [IC, 4, T])
        s_h = sb("s_h", [IC, 4, NT])
        s_th = sb("s_th", [IC, 2, 512])
        s_gg = sb("s_gg", [IC, 2, 512])
        w1_sb = sb("w1_sb", [P, 4, TC, 2 * IC])
        w2_sb = sb("w2_sb", [P, 4, 2, T])
        y6 = sb("y6", [P, 4, K, T])
        onehot = sb("onehot", [P, 2, B, P], F16)
        rows = sb("rows", [P, 4, T])
        xe = sb("xe", [P, 2, TC, P])
        th = sb("th", [IC, 2, 2 * P])
        hs = sb("hs", [IC, 2, 2, P])
        y_sb = sb("y_sb", [P, 4, T])
        logits = sb("logits", [P, B, E])
        eq = sb("eq", [P, B, E])
        rank = sb("rank", [P, B, E])
        chosen = sb("chosen", [P, B, E], F16)
        far = sb("far", [P, B, E])

        def ps(name, banks):
            return es.enter_context(nc.psum_tensor(name, [P, 512 * banks], F32))

        b0, b1 = ps("b0", 1), ps("b1", 1)
        score = [ps("score0", 2), ps("score1", 2)]
        b6, b7 = ps("b6", 1), ps("b7", 1)
        bank = [b0[:, :], b1[:, :], score[0][:, 0:512], score[0][:, 512:1024], score[1][:, 0:512],
                score[1][:, 512:1024], b6[:, :], b7[:, :]]

        ld_x, ld_ctx, ld_w, ld_small, ld_mask, ld_bc, ld_gate, ld_shared = [sem(n) for n in (
            "ld_x", "ld_ctx", "ld_w", "ld_small", "ld_mask", "ld_bc", "ld_gate", "ld_shared")]
        consts = sem("consts")
        zeroed = [sem(f"zeroed{n}") for n in range(3)]
        zero_col = sem("zero_col")
        ones_done = sem("ones_done")
        ones_in = sem("ones_in")
        dv = sem("dv")
        av = sem("av")
        pl = sem("pl")
        pool_steps = sem("pool_steps")
        var_done = sem("var_done")
        rstd_done = sem("rstd_done")
        normed = sem("normed")
        proj = sem("proj")
        taken = sem("taken")
        mask_col = sem("mask_col")
        aug = sem("aug")
        fulls = sem("fulls")
        highs = sem("highs")
        lows = sem("lows")
        parts_out = [sem(f"parts_out{n}") for n in range(B)]
        aug_out = sem("aug_out")
        stack_in = [sem(f"stack_in{n}") for n in range(3)]
        max_out = sem("max_out")
        max_in = sem("max_in")
        a_done, max_done, b_done, exp_done, pv_done, os_done, t_ready, nm_done, v_ready, on_done, x1_done = [
            sem(n) for n in ("a_done", "max_done", "b_done", "exp_done", "pv_done", "os_done", "t_ready",
                             "nm_done", "v_ready", "on_done", "x1_done")]
        tanh_g = sem("tanh_g")
        tok_normed, tok_out, xt_ready, xt_done, lg_ready, lg_done = [sem(n) for n in (
            "tok_normed", "tok_out", "xt_ready", "xt_done", "lg_ready", "lg_done")]
        soft, softd, chosen_done, pos_ready, cnt_ready, beg_in, beg_ready, plan_in, plan_ready, plan_done, route_done = [
            sem(n) for n in ("soft", "softd", "chosen_done", "pos_ready", "cnt_ready", "beg_in", "beg_ready",
                             "plan_in", "plan_ready", "plan_done", "route_done")]
        sg_ready, sth_done, sh_done, sdn_ready, acc_done = [sem(n) for n in (
            "sg_ready", "sth_done", "sh_done", "sdn_ready", "acc_done")]
        pick_done, hot, inv, idx, xpose, xe_done, s1, th_done, hs_done, s2, y_done = [sem(n) for n in (
            "pick_done", "hot", "inv", "idx", "xpose", "xe_done", "s1", "th_done", "hs_done", "s2", "y_done")]
        w_in = [sem(f"w_in{n}") for n in range(4)]
        rows_in = [sem(f"rows_in{n}") for n in range(4)]
        y_out = [sem(f"y_out{n}") for n in range(4)]
        (v_w, v_pick, v_hot, v_inv, v_idx, v_rows, v_x, v_xe, v_s1, v_th, v_hs, v_s2, v_y, v_out, v_free) = [
            sem(f"over_{n}") for n in ("w", "pick", "hot", "inv", "idx", "rows", "x", "xe", "s1", "th", "hs", "s2", "y", "out",
                                       "free")]
        y6_in = [sem(f"y6_in{n}") for n in range(4)]
        scattered, stored = sem("scattered"), sem("stored")
        mixed = [sem("mixed_dve"), sem("mixed_act")]
        weighted, summed = sem("weighted"), sem("summed")

        block = es.enter_context(nc.Block())

        NA = B * H
        LAG = 24
        NP = NA // 2
        NG = NA // 4

        def pair_at(a):
            return (a - LAG) // 2 if a >= LAG and (a - LAG) % 2 == 0 else -1

        def pair_of(a):
            p = pair_at(a)
            return p if 0 <= p < NP else None

        def group_of(a):
            p = pair_at(a)
            return (p - 3) // 2 if p >= 3 and p % 2 == 1 and (p - 3) // 2 < NG else None

        events = {}
        for b in range(B):
            events.setdefault(16 * b + 17, []).append(("max", b, 0))
            events.setdefault(16 * b + 45, []).append(("out", b, 0))
            events.setdefault(16 * b + 47, []).append(("out", b, 1))
            events.setdefault(16 * b + 51, []).append(("back", b, 0))
        STEPS = 16 * (B - 1) + 54
        t_index = {e: n for n, e in enumerate(e for a in sorted(events) for e in events[a])}

        L_PICK, L_HOT, L_INV, L_IDX, L_GATHER, L_X, L_S1 = 8, 7, 7, 6, 5, 3, 2
        U = 8
        LOOP = range(1, 7)

        class Ex:

            def __init__(self, q, r):
                self.q, self.r = q + r // U if r >= U or r < 0 else q, r % U
                self.v = self.q * U + self.r

            def use(self, ring):
                return self.q * (U // ring) + self.r // ring

        shared_at = {-8: (("up", 5), ("up", 6)), -7: (("up", 7), ("down", 0)),
                     -6: (("down", 1), ("down", 2), ("down", 3)), -5: (("down", 4), ("down", 5)),
                     -4: (("down", 6), ("down", 7))}

        def experts(eng, stages, shared={}):
            def step(q, r, check):
                for lead, f in stages:
                    e = Ex(q, r + lead)
                    if not check or 0 <= e.v < TILES:
                        f(e)

            for n in range(-L_PICK, U):
                step(0, n, True)
                for kind, j in shared_at.get(n, ()):
                    if kind in shared:
                        shared[kind](j)
            with eng.Fori(LOOP.start, LOOP.stop) as q:
                for r in range(U):
                    step(q, r, False)
            for n in range(U * LOOP.stop, TILES):
                step(0, n, True)

        def expert_of(e, over):
            return over[e.v - E] if isinstance(e.v, int) and e.v >= E else e.v

        def first(e, n):
            return isinstance(e.v, int) and e.v < n

        ON_PE = (1, 4, 6)

        def mixed_by(b):
            side = b in ON_PE
            return mixed[side], sum((b2 in ON_PE) == side for b2 in range(b + 1))

        @block.sync
        def _(sp):
            sp.dma_start(ctx_sb[:, :, :], ctx_in).then_inc(ld_ctx, 16)
            for n, w in enumerate((wk, wq, wv)):
                sp.dma_start(w_sb[:, n, :], w).then_inc(ld_w, 16)
            sp.dma_start(x_sb[:, :, :], x).then_inc(ld_x, 16)
            sp.dma_start(mask_bc[:, :], mask.rearrange("(o b) t -> o (b t)", o=1).to_broadcast([P, B * T])).then_inc(ld_bc, 16)
            sp.dma_start(gate_sb[:, :, :], gate).then_inc(ld_gate, 16)
            sp.wait_ge(aug, 4)
            for parts, m in ((q_parts, 0), (k_parts, 2)):
                for hl in range(2):
                    dst = parts[:, hl, D * H:HD1 * H, :]
                    sp.dma_start(dst, mask_hl[:, m + hl:m + hl + 1, :].bitcast(F32).to_broadcast([B, H, T])).then_inc(aug_out, 16)
            sp.wait_ge(ones_done, 1)
            for s in range(3):
                sp.dma_start(k_st[s][AROWS:BROWS, :, :].bitcast(F32),
                             ones_st[:, :].rearrange("p (o t) -> p o t", o=1).to_broadcast([2, H, T])).then_inc(ones_in, 16)

            def send_parts(j):
                parts, n = (q_parts if j % 2 else k_parts), j // 2
                for hl, (t, done) in enumerate(((high, highs), (low, lows))):
                    sp.wait_ge(done, j + 1)
                    dst = parts[2 * n:2 * n + 2, hl, 0:D * H, :].rearrange("b p t -> p b t")
                    sp.dma_start(dst, t[:, j % 2, :].bitcast(F32).rearrange("p (b t) -> p b t", b=2)).then_inc(parts_out[j], 16)

            def load_stacks(b):
                s, use = b % 3, stack_in[b % 3]
                sp.wait_ge(parts_out[b // 2 * 2], 32)
                sp.wait_ge(parts_out[b // 2 * 2 + 1], 32)
                if b == 0:
                    sp.wait_ge(aug_out, 64)
                if b < 3:
                    sp.wait_ge(zeroed[b], 2)
                if b >= 3:
                    sp.wait_ge(b_done, 8 * (b - 2))
                qp = q_parts[b].rearrange("l (d h) t -> (l d) (h t)", h=H)
                kp = k_parts[b].rearrange("l (d h) t -> (l d) (h t)", h=H)
                flatq = q_st[s][:, :, :].bitcast(F32).rearrange("p h t -> p (h t)")
                flatk = k_st[s][:, :, :].bitcast(F32).rearrange("p h t -> p (h t)")
                sp.dma_start(flatq[0:PART, :], qp).then_inc(use, 16)
                sp.dma_start(flatq[PART:SROWS, :], qp).then_inc(use, 16)
                sp.dma_start(flatk[0:PART, :], kp).then_inc(use, 16)
                sp.dma_start(flatk[PART:PART + HD1, :], kp[HD1:PART, :]).then_inc(use, 16)
                sp.dma_start(flatk[PART + HD1:SROWS, :], kp[0:HD1, :]).then_inc(use, 16)

            def send_max(b):
                sp.wait_ge(nm_done, 2 * (b + 1))
                for hl in range(2):
                    sp.dma_start(max_parts[b, hl], nm[:, b % 2, hl, :].bitcast(F32)).then_inc(max_out, 16)
                sp.wait_ge(max_out, 32 * (b + 1))
                flatq = q_st[b % 3][:, :, :].bitcast(F32).rearrange("p h t -> p (h t)")
                sp.dma_start(flatq[AROWS:BROWS, :], max_parts[b].rearrange("l h t -> l (h t)")).then_inc(max_in, 16)

            for j in range(B):
                send_parts(j)
                if j in (2, 3, 6):
                    load_stacks((2, 3, 6).index(j))
            for b in range(B):
                send_max(b)
                if 1 <= b and b + 2 < B:
                    load_stacks(b + 2)
            sp.wait_ge(b_done, NP)
            sp.dma_start(sgu_sb[:, :, :, :], sgu).then_inc(ld_shared, 16)
            sp.dma_start(sd_sb[:, :, :], sd).then_inc(ld_shared, 16)
            for b in range(B):
                sp.wait_ge(tok_normed, b + 1)
                sp.dma_start(tokens[b * P:(b + 1) * P, :], xn[:, b, :]).then_inc(tok_out, 16)

            over = ()

            def load_weights(e):
                r = e.r % 4
                if not first(e, 4):
                    sp.wait_ge(s2, e.v - 3)
                sp.dma_start(w1_sb[:, r, :, :], w1[bass.ds(expert_of(e, over), 1)].rearrange("o p k i -> p (o k) i")).then_inc(w_in[r], 16)
                sp.dma_start(w2_sb[:, r, :, :], w2[bass.ds(expert_of(e, over), 1)].rearrange("o p c t -> p (o c) t")).then_inc(w_in[r], 16)

            for e in range(3):
                load_weights(Ex(0, e))

            def load_later(e):
                if not first(e, 3):
                    load_weights(e)

            sp.wait_ge(plan_done, 1)
            over = [sp.value_load(plan[0:1, i:i + 1], min_val=0, max_val=E - 1) for i in range(OVER)]
            experts(sp, [(3, load_later)])
            n_over = sp.value_load(plan[0:1, 2 * NOV:2 * NOV + 1], min_val=0, max_val=NOV)
            sp.wait_ge(s2, TILES)
            with sp.If(n_over > OVER):
                with sp.Fori(0, n_over - OVER) as i:
                    e = sp.value_load(plan[0:1, bass.ds(i + OVER, 1)], min_val=0, max_val=E - 1)
                    sp.wait_ge(v_s2, i + 1)
                    sp.dma_start(w1_sb[:, 0, :, :], w1[bass.ds(e, 1)].rearrange("o p k i -> p (o k) i")).then_inc(v_w, 16)
                    sp.dma_start(w2_sb[:, 0, :, :], w2[bass.ds(e, 1)].rearrange("o p c t -> p (o c) t")).then_inc(v_w, 16)
            with sp.Else():
                sp.nop()
            sp.wait_ge(scattered, 1)
            for b in range(B):
                if b >= 4:
                    sp.wait_ge(*mixed_by(b - 4))
                src = routed[b * P * K:(b + 1) * P * K, :].rearrange("(p k) t -> p k t", k=K)
                sp.dma_start(y6[:, b % 4, :, :], src).then_inc(y6_in[b % 4], 16)
            for b in range(B):
                sp.wait_ge(*mixed_by(b))
                sp.dma_start(out[:, b, :], x_sb[:, b, :]).then_inc(stored, 16)
            sp.wait_ge(stored, 16 * B)

        @block.gpsimd
        def _(pool):
            n = [0]

            def link(ins):
                n[0] += 1
                ins.then_inc(pl, 1)
                pool.wait_ge(pl, n[0])

            pool.memset(zeros[:], 0.0).then_inc(zero_col, 1)
            pool.memset(ones_st[:], 1.0).then_inc(ones_done, 1)
            link(pool.memset(ident[:], 0.0))
            link(pool.affine_select(out=ident[:], in_=ident[:], compare_op=ALU.not_equal, fill=1.0, base=0,
                                    pattern=[[-1, P]], channel_multiplier=1))
            pool.memset(ones16[:], 1.0).then_inc(consts, 1)
            link(pool.memset(tri[:], 1.0))
            link(pool.affine_select(out=tri[:], in_=tri[:], compare_op=ALU.is_gt, fill=0.0, base=0,
                                    pattern=[[1, P]], channel_multiplier=-1))
            link(pool.memset(tri_f[:], 1.0))
            link(pool.affine_select(out=tri_f[:], in_=tri_f[:], compare_op=ALU.is_gt, fill=0.0, base=0,
                                    pattern=[[1, E]], channel_multiplier=-1))
            link(pool.memset(ones_f[:], 1.0))
            link(pool.memset(neg_half[:], -0.5))
            link(pool.memset(v_pad[:, :, :, :, :], 0.0))
            link(pool.memset(v_pad[:, :, :, :, D:D + 1], 1.0))
            pool.iota(iota_e[:], pattern=[[1, E]], base=0, channel_multiplier=0, allow_small_or_imprecise_dtypes=True).then_inc(consts, 1)
            pool.iota(iota_w[:], pattern=[[1, NT + P]], base=0, channel_multiplier=0, allow_small_or_imprecise_dtypes=True).then_inc(consts, 1)
            pool.iota(iota_t[:], pattern=[[P, B]], base=0, channel_multiplier=1, allow_small_or_imprecise_dtypes=True).then_inc(consts, 1)
            pool.iota(iota_p[:], pattern=[[0, 1]], base=0, channel_multiplier=1, allow_small_or_imprecise_dtypes=True).then_inc(consts, 1)
            pool.iota(low6[:], pattern=[[0, 1]], base=-1, channel_multiplier=K, allow_small_or_imprecise_dtypes=True).then_inc(consts, 1)
            pool.iota(c128[:], pattern=[[P, 7]], base=P, channel_multiplier=0, allow_small_or_imprecise_dtypes=True).then_inc(consts, 1)
            pool.iota(iota_q[:], pattern=[[1, NOV]], base=0, channel_multiplier=0, allow_small_or_imprecise_dtypes=True).then_inc(consts, 1)
            pool.wait_ge(consts, 8)
            pool.sem_inc(consts, 1)

            for st in (q_st[1], k_st[1]):
                pool.memset(st[0:AROWS, :, :].bitcast(F32), 0.0).then_inc(zeroed[1], 1)

            pool.wait_ge(var_done, 1)
            pool.tensor_tensor(rstd[:, :], var[:, :], neg_half[:, :], ALU.pow).then_inc(rstd_done, 1)

            for j in range(B):
                pool.wait_ge(highs, j + 1)
                if j >= 2:
                    m = j - 2
                    pool.wait_ge(parts_out[m], 32)
                pool.tensor_tensor(low[:, j % 2, :], full[:, j % 2, :], high[:, j % 2, :].bitcast(F32), ALU.subtract).then_inc(lows, 1)

            pool.wait_ge(taken, 4)
            pool.wait_ge(mask_col, 1)
            for b in range(B):
                if b >= 2:
                    pool.wait_ge(pv_done, 4 * (b - 1))
                for s in range(TC):
                    last = pool.tensor_scalar(v_pad[:, b % 2, s, :, 0:D],
                                              vals[:, b * TC + s, :].rearrange("p (h d) -> p h d", d=D),
                                              mask_c[:, b * TC + s:b * TC + s + 1], None, ALU.mult)
                last.then_inc(v_ready, 1)

            pool.wait_ge(var_done, 2)
            pool.tensor_tensor(rstd[:, :], var[:, :], neg_half[:, :], ALU.pow).then_inc(rstd_done, 1)
            pool.wait_ge(tok_out, 16 * B)

            def gather(e):
                pool.wait_ge(idx, e.v + 1)
                if not first(e, 4):
                    pool.wait_ge(xpose, e.v - 3)
                pool.sem_inc(pool_steps, 1)
                pool.indirect_dma_start(
                    out=rows[:, e.r % 4, :], out_offset=None, in_=tokens,
                    in_offset=bass.IndirectOffsetOnAxis(ap=g_idx[:, e.r:e.r + 1], axis=0)).then_inc(rows_in[e.r % 4], 16)

            def scatter(e):
                pool.wait_ge(y_done, e.v + 1)
                pool.sem_inc(pool_steps, 1)
                pool.indirect_dma_start(
                    out=routed, out_offset=bass.IndirectOffsetOnAxis(ap=s_idx[:, e.r:e.r + 1], axis=0),
                    in_=y_sb[:, e.r % 4, :], in_offset=None, bounds_check=NT * K - 1,
                    oob_is_err=False).then_inc(y_out[e.r % 4], 16)

            experts(pool, [(0, scatter), (L_GATHER, gather)])
            pool.wait_ge(plan_done, 1)
            n_over = pool.value_load(plan[0:1, 2 * NOV:2 * NOV + 1], min_val=0, max_val=NOV)
            for r in range(4):
                pool.wait_ge(y_out[r], 16 * ((TILES - r + 3) // 4))
            pool.sem_inc(v_free, 1)
            with pool.If(n_over > OVER):
                with pool.Fori(0, n_over - OVER) as i:
                    pool.wait_ge(v_idx, i + 1)
                    pool.sem_inc(pool_steps, 1)
                    pool.indirect_dma_start(
                        out=rows[:, 0, :], out_offset=None, in_=tokens,
                        in_offset=bass.IndirectOffsetOnAxis(ap=g_idx[:, 0:1], axis=0)).then_inc(v_rows, 16)
                    pool.wait_ge(v_y, i + 1)
                    pool.sem_inc(pool_steps, 1)
                    pool.indirect_dma_start(
                        out=routed, out_offset=bass.IndirectOffsetOnAxis(ap=s_idx[:, 0:1], axis=0),
                        in_=y_sb[:, 0, :], in_offset=None, bounds_check=NT * K - 1,
                        oob_is_err=False).then_inc(v_out, 16)
                    pool.wait_ge(v_out, 16 * i + 16)
                    pool.sem_inc(v_free, 1)
            with pool.Else():
                pool.nop()
            pool.sem_inc(scattered, 1)

        @block.scalar
        def _(act):
            act.dma_start(mask_r[:, :], mask.rearrange("b (s p) -> (b s) p", p=P)).then_inc(ld_mask, 16)
            act.dma_start(mask_b[:, :], mask).then_inc(ld_mask, 16)
            act.dma_start(b_sb[:, 0:1], bk).then_inc(ld_small, 16)
            act.dma_start(b_sb[:, 1:2], bq).then_inc(ld_small, 16)
            act.dma_start(bv_sb[:, :], bv.to_broadcast([P, P])).then_inc(ld_small, 16)
            act.dma_start(g_sb[:, 0:1], g_xattn.to_broadcast([P, 1])).then_inc(ld_small, 16)
            act.dma_start(g_sb[:, 1:2], g_ffn.to_broadcast([P, 1])).then_inc(ld_small, 16)
            act.wait_ge(zero_col, 1)
            for st in (q_st[2], k_st[2]):
                act.activation(st[0:AROWS, :, :].rearrange("p h t -> p (h t)"),
                               zeros[0:AROWS, :].to_broadcast([AROWS, H * T]), ACT.Copy).then_inc(zeroed[2], 1)
            act.wait_ge(ld_small, 80)
            act.activation(tg[:, 0:2], g_sb[:, :], ACT.Tanh).then_inc(tanh_g, 1)
            for j in range(B):
                act.wait_ge(fulls, j + 1)
                if j >= 2:
                    act.wait_ge(parts_out[j - 2], 32)
                act.activation(high[:, j % 2, :], full[:, j % 2, :], ACT.Copy).then_inc(highs, 1)

            for a in range(STEPS + 2):
                p = pair_of(a)
                if p is not None:
                    act.wait_ge(b_done, p + 1)
                    if p >= 4:
                        act.wait_ge(pv_done, (p - 4) // 2 + 1)
                    act.activation(probs[:, p % 4, 0:1024], score[p % 2][:, :], ACT.Exp, scale=1.0 / ROOT).then_inc(exp_done, 1)
                gq = group_of(a - 1)
                if gq is not None:
                    b, g = divmod(gq, 4)
                    act.wait_ge(pv_done, gq + 1)
                    if b >= 2 and g == 0:
                        act.wait_ge(x1_done, b - 1)
                    act.activation(o_sb[:, b % 2, g, :], bank[6][:, 0:T], ACT.Copy).then_inc(os_done, 1)

            for b in range(B):
                act.wait_ge(xt_ready, b + 1)
                act.activation(xt[:, :, b * P:(b + 1) * P], bank[b % 2][:, 0:TC * P].rearrange("p (k n) -> p k n", k=TC),
                               ACT.Copy).then_inc(xt_done, 1)
            act.wait_ge(lg_ready, 1)
            act.activation(logits[:, :, :], bank[2][:, 0:B * E].rearrange("p (b e) -> p b e", b=B), ACT.Copy).then_inc(lg_done, 1)
            act.wait_ge(soft, 1)
            act.activation(e6[:, :, :], e6[:, :, :], ACT.Exp).then_inc(softd, 1)

            def shared_tanh(j):
                act.wait_ge(sg_ready, j + 1)
                if j >= 2:
                    act.wait_ge(sh_done, j - 1)
                act.activation(s_th[:, j % 2, :], bank[3 + 2 * (j % 2)][0:IC, :], ACT.Tanh, scale=0.5).then_inc(sth_done, 1)

            for j in range(5):
                shared_tanh(j)

            def pick(e):
                if not first(e, 4):
                    act.wait_ge(inv, e.v - 3)
                act.activation(picked[:, e.r % 4, :, :], route[:, :, bass.ds(expert_of(e, over), 1), :].rearrange("p b o n -> p b (o n)"),
                               ACT.Copy).then_inc(pick_done, 1)

            def take_x(e):
                act.wait_ge(xpose, e.v + 1)
                if not first(e, 2):
                    act.wait_ge(s1, e.v - 1)
                act.activation(xe[:, e.r % 2, :, :], bank[1 + e.r % 2][:, 0:TC * P].rearrange("p (k n) -> p k n", k=TC),
                               ACT.Copy).then_inc(xe_done, 1)

            def tanh(e):
                act.wait_ge(s1, e.v + 1)
                if not first(e, 2):
                    act.wait_ge(hs_done, e.v - 1)
                act.activation(th[:, e.r % 2, :], bank[3 + e.r % 2][0:IC, 0:2 * P], ACT.Tanh, scale=0.5).then_inc(th_done, 1)

            def take_y(e):
                act.wait_ge(s2, e.v + 1)
                if not first(e, 4):
                    act.wait_ge(y_out[e.r % 4], 16 * e.use(4))
                act.activation(y_sb[:, e.r % 4, :], bank[5 + e.r % 2][:, 0:T], ACT.Copy).then_inc(y_done, 1)

            def take_sum(n):
                act.wait_ge(summed, n + 1)
                act.activation(x_sb[:, ON_PE[n], :], bank[n % 2][:, 0:T], ACT.Copy).then_inc(mixed[1], 1)

            act.wait_ge(route_done, 1)
            act.wait_ge(plan_done, 1)
            over = [act.value_load(plan[0:1, i:i + 1], min_val=0, max_val=E - 1) for i in range(OVER)]
            experts(act, [(L_PICK, pick), (0, take_y), (L_S1, tanh), (L_X, take_x)], {"up": shared_tanh})
            act.wait_ge(plan_done, 1)
            n_over = act.value_load(plan[0:1, 2 * NOV:2 * NOV + 1], min_val=0, max_val=NOV)
            for r in range(4):
                act.wait_ge(y_out[r], 16 * ((TILES - r + 3) // 4))
            with act.If(n_over > OVER):
                with act.Fori(0, n_over - OVER) as i:
                    e = act.value_load(plan[0:1, bass.ds(i + OVER, 1)], min_val=0, max_val=E - 1)
                    act.activation(picked[:, 0, :, :], route[:, :, bass.ds(e, 1), :].rearrange("p b o n -> p b (o n)"),
                                   ACT.Copy).then_inc(v_pick, 1)
                    act.wait_ge(v_x, i + 1)
                    act.activation(xe[:, 0, :, :], bank[1][:, 0:TC * P].rearrange("p (k n) -> p k n", k=TC),
                                   ACT.Copy).then_inc(v_xe, 1)
                    act.wait_ge(v_s1, i + 1)
                    act.activation(th[:, 0, :], bank[3][0:IC, 0:2 * P], ACT.Tanh, scale=0.5).then_inc(v_th, 1)
                    act.wait_ge(v_s2, i + 2)
                    act.wait_ge(v_free, i + 1)
                    act.activation(y_sb[:, 0, :], bank[5][:, 0:T], ACT.Copy).then_inc(v_y, 1)
            with act.Else():
                act.nop()
            for n, b in enumerate(ON_PE):
                act.wait_ge(y6_in[b % 4], 16 * (b // 4 + 1))
                for k in range(K):
                    last = act.activation(y6[:, b % 4, k, :], y6[:, b % 4, k, :], ACT.Copy, scale=ww[:, b, k:k + 1])
                last.then_inc(weighted, 1)
                if n:
                    take_sum(n - 1)
            take_sum(len(ON_PE) - 1)

        @block.vector
        def _(dve):
            n = [0]

            def link(ins):
                n[0] += 1
                ins.then_inc(dv, 1)
                dve.wait_ge(dv, n[0])

            for st in (q_st[0], k_st[0]):
                dve.memset(st[0:AROWS, :, :].bitcast(F32), 0.0).then_inc(zeroed[0], 1)
            dve.wait_ge(ld_mask, 32)
            link(dve.tensor_scalar(mask_k[:, :], mask_b[:, :], NEG * ROOT, -NEG * ROOT, ALU.mult, ALU.add))
            for m, src in enumerate((mask_b, mask_k)):
                dve.tensor_copy(mask_hl[:, 2 * m, :], src[:, :]).then_inc(aug, 1)
                dve.wait_ge(aug, 2 * m + 1)
                dve.tensor_tensor(mask_hl[:, 2 * m + 1, :], src[:, :], mask_hl[:, 2 * m, :].bitcast(F32), ALU.subtract).then_inc(aug, 1)
            dve.wait_ge(proj, 1)
            dve.tensor_copy(mask_c[:, :], bank[0][:, 0:B * TC]).then_inc(mask_col, 1)

            def variances():
                for b in range(B):
                    last = dve.bn_stats(stats[:, b, :], x_sb[:, b, :])
                link(last)
                for b in range(B):
                    last = dve.bn_aggr(mv[:, b, :], stats[:, b, :])
                link(last)
                dve.tensor_scalar(var[:, :], mv[:, :, 1], EPS, None, ALU.add).then_inc(var_done, 1)

            def normalize(bs, done):
                for b in bs:
                    dve.tensor_scalar(xn[:, b, :], x_sb[:, b, :], mv[:, b, 0:1], rstd[:, b:b + 1],
                                      ALU.subtract, ALU.mult).then_inc(done, 1)

            dve.wait_ge(ld_x, 16)
            variances()
            dve.wait_ge(ld_small, 80)
            dve.wait_ge(ld_bc, 16)
            for j in range(B):
                if j % 2:
                    dve.wait_ge(rstd_done, 1)
                    normalize((j - 1, j), normed)
                dve.wait_ge(proj, j + 2)
                if j >= 2:
                    dve.wait_ge(lows, j - 1)
                c = (j // 2) * 2 * T
                dve.scalar_tensor_tensor(full[:, j % 2, :], bank[(j + 1) % 8], b_sb[:, j % 2:j % 2 + 1],
                                         mask_bc[:, c:c + 2 * T], ALU.add, ALU.mult).then_inc(fulls, 1)
            for j in range(4):
                dve.wait_ge(proj, 10 + j)
                dve.tensor_tensor(vals[:, 4 * j:4 * j + 4, :], bank[(j + 1) % 8].rearrange("p (s n) -> p s n", s=4),
                                  bv_sb[:, :].rearrange("p (o n) -> p o n", o=1).to_broadcast([P, 4, P]), ALU.add).then_inc(taken, 1)
            dve.wait_ge(tanh_g, 1)
            dve.wait_ge(mask_col, 1)

            t_seen = 0
            for a in range(STEPS + 2):
                if a < NA:
                    dve.wait_ge(a_done, a + 1)
                    b, h = divmod(a, H)
                    if b >= 2 and h == 0:
                        dve.wait_ge(t_ready, t_index[("max", b - 2, 0)] + 1)
                    dve.tensor_reduce(mx[:, b % 2, :, h], bank[a % 2].rearrange("p (c s) -> p c s", c=TC),
                                      AX.X, ALU.max).then_inc(max_done, 1)
                for kind, b, c in events.get(a - 1, []):
                    t_seen += 1
                    dve.wait_ge(t_ready, t_seen)
                    if kind == "max":
                        if b >= 2:
                            dve.wait_ge(max_out, 32 * (b - 1))
                        src = bank[7][0:H, 0:T]
                        dve.tensor_scalar(nm[:, b % 2, 0, :], src, -1.0, None, ALU.mult).then_inc(nm_done, 1)
                        dve.wait_ge(nm_done, 2 * b + 1)
                        dve.scalar_tensor_tensor(nm[:, b % 2, 1, :], src, -1.0, nm[:, b % 2, 0, :].bitcast(F32),
                                                 ALU.mult, ALU.subtract).then_inc(nm_done, 1)
                    elif kind == "out":
                        src = bank[7].rearrange("p (h r) -> p h r", r=32)
                        link(dve.reciprocal(rz[:, 0, :], src[:, :, D]))
                        link(dve.tensor_scalar(rz[:, 1, :], rz[:, 0, :], mask_c[:, b * TC + c:b * TC + c + 1], None, ALU.mult))
                        dve.tensor_tensor(o_n[:, c, :].rearrange("p (h d) -> p h d", d=D), src[:, :, 0:D],
                                          rz[:, 1, :].rearrange("p (h o) -> p h o", o=1).to_broadcast([P, H, D]),
                                          ALU.mult).then_inc(on_done, 1)
                    else:
                        dve.scalar_tensor_tensor(x_sb[:, b, :], bank[7][:, 0:T], tg[:, 0:1], x_sb[:, b, :],
                                                 ALU.mult, ALU.add).then_inc(x1_done, 1)

            dve.wait_ge(x1_done, B)
            variances()
            dve.wait_ge(rstd_done, 2)
            normalize(range(B), tok_normed)
            dve.tensor_scalar(tg[:, 2:3], tg[:, 1:2], 0.5, None, ALU.mult)
            dve.wait_ge(lg_done, 1)
            for b in range(B):
                last = dve.max(v8[:, b, :], logits[:, b, :])
            link(last)
            for b in range(B):
                last = dve.max_index(i8[:, b, :], v8[:, b, :], logits[:, b, :])
            link(last)
            dve.tensor_tensor(e6[:, :, :], v8[:, :, 0:K], v8[:, :, 0:1].to_broadcast([P, B, K]), ALU.subtract).then_inc(soft, 1)
            link(dve.tensor_copy(if8[:, :, :], i8[:, :, :]))
            dve.wait_ge(consts, 9)

            def shared_hidden(j):
                g_ps, u_ps = bank[3 + 2 * (j % 2)][0:IC, :], bank[3 + 2 * (j % 2) + 1][0:IC, :]
                nb, c = divmod(j, 4)
                dve.wait_ge(sth_done, j + 1)
                link(dve.scalar_tensor_tensor(s_gg[:, j % 2, :], s_th[:, j % 2, :], 1.0, g_ps, ALU.add, ALU.mult))
                dve.tensor_tensor(s_h[:, c, nb * 512:(nb + 1) * 512], s_gg[:, j % 2, :], u_ps, ALU.mult).then_inc(sh_done, 1)

            def shared_add(b):
                dve.wait_ge(sdn_ready, b + 1)
                dve.scalar_tensor_tensor(x_sb[:, b, :], bank[1 + b % 2][:, 0:T], tg[:, 2:3], x_sb[:, b, :],
                                         ALU.mult, ALU.add).then_inc(acc_done, 1)

            for k in range(K):
                dst = rank if k == 0 else eq
                link(dve.tensor_tensor(dst[:, :, :], iota_e[:, :].rearrange("p (o e) -> p o e", o=1).to_broadcast([P, B, E]),
                                       if8[:, :, k:k + 1].to_broadcast([P, B, E]), ALU.is_equal))
                if k:
                    link(dve.scalar_tensor_tensor(rank[:, :, :], eq[:, :, :], float(k + 1), rank[:, :, :], ALU.mult, ALU.add))
                if k in (1, 4):
                    shared_hidden(k // 4)
            dve.tensor_scalar(chosen[:, :, :], rank[:, :, :], 1.0, None, ALU.min).then_inc(chosen_done, 1)
            dve.tensor_scalar(far[:, :, :], rank[:, :, :], 1.0, None, ALU.min)
            for b in range(B):
                dve.memset(route[:, b, :, 2], float(K * P * b - FAR))
                dve.tensor_scalar(route[:, b, :, 1], iota_e[:, :], 0.0, iota_t[:, b:b + 1], ALU.mult, ALU.add)
            link(dve.tensor_scalar(route[:, :, :, 3], rank[:, :, :], low6[:, 0:1], None, ALU.add))
            link(dve.tensor_scalar(far[:, :, :], far[:, :, :], float(FAR), -float(FAR), ALU.mult, ALU.add))
            shared_hidden(2)
            dve.wait_ge(pos_ready, 1)
            dve.tensor_tensor(route[:, :, :, 0], bank[7].rearrange("p (b e) -> p b e", b=B), far[:, :, :], ALU.add).then_inc(route_done, 1)
            dve.wait_ge(softd, 1)
            link(dve.tensor_reduce(e6s[:, :], e6[:, :, :], AX.X, ALU.add))
            link(dve.reciprocal(e6s[:, :], e6s[:, :]))
            link(dve.tensor_scalar(e6s[:, :], e6s[:, :], tg[:, 2:3], None, ALU.mult))
            dve.tensor_tensor(ww[:, :, :], e6[:, :, :], e6s[:, :].rearrange("p (b o) -> p b o", o=1).to_broadcast([P, B, K]), ALU.mult)
            dve.wait_ge(cnt_ready, 1)
            link(dve.tensor_copy(n_e[:, :], bank[2][0:E, 0:1]))
            link(dve.tensor_scalar(c_tmp[:, :], c128[:, :], n_e[:, 0:1], None, ALU.is_lt))
            dve.tensor_reduce(extra[:, :], c_tmp[:, :], AX.X, ALU.add).then_inc(beg_in, 1)
            shared_hidden(3)
            dve.wait_ge(beg_ready, 1)
            link(dve.tensor_copy(o_beg[:, :], bank[2][0:E, 8:9]))
            link(dve.tensor_tensor(o_end[:, :], o_beg[:, :], extra[:, :], ALU.add))
            link(dve.tensor_scalar(t_ge[:, :], iota_q[:, :], o_beg[:, 0:1], None, ALU.is_ge))
            link(dve.scalar_tensor_tensor(t_in[:, :], iota_q[:, :], o_end[:, 0:1], t_ge[:, :], ALU.is_lt, ALU.mult))
            link(dve.tensor_scalar(t_c[:, :], iota_q[:, :], o_beg[:, 0:1], 1.0 - B, ALU.subtract, ALU.add))
            dve.tensor_tensor(t_c2[:, :], t_c[:, :], t_in[:, :], ALU.mult).then_inc(plan_in, 1)
            shared_hidden(4)
            dve.wait_ge(plan_ready, 1)
            src = bank[2][0:1, 16:16 + 2 * NOV + 1]
            dve.tensor_copy(plan[0:1, 0:NOV], src[:, 0:NOV])
            dve.tensor_scalar(plan[0:1, NOV:2 * NOV], src[:, NOV:2 * NOV], float(B), None, ALU.add)
            dve.tensor_copy(plan[0:1, 2 * NOV:2 * NOV + 1], src[:, 2 * NOV:2 * NOV + 1]).then_inc(plan_done, 1)

            def hot_rows(e):
                dve.wait_ge(pick_done, e.v + 1)
                if not first(e, 2):
                    dve.wait_ge(inv, e.v - 1)
                base = chunks[e.v - E] * P if isinstance(e.v, int) and e.v >= E else 0
                dve.tensor_tensor(onehot[:, e.r % 2, :, :],
                                  iota_w[:, bass.ds(base, P)].rearrange("p (o j) -> p o j", o=1).to_broadcast([P, B, P]),
                                  picked[:, e.r % 4, :, 0:1].to_broadcast([P, B, P]), ALU.is_equal).then_inc(hot, 1)

            def indices(e):
                dve.wait_ge(inv, e.v + 1)
                if not first(e, 8):
                    dve.wait_ge(y_out[e.r % 4], 16 * (e.use(4) - 1))
                src = bank[7 * (e.r % 2)][:, 0:3]
                dve.tensor_copy(g_idx[:, e.r:e.r + 1], src[:, 0:1])
                dve.tensor_scalar(s_idx[:, e.r:e.r + 1], src[:, 1:2], float(FAR), src[:, 2:3],
                                  ALU.add, ALU.add).then_inc(idx, 1)

            def hidden(e):
                dve.wait_ge(th_done, e.v + 1)
                if not first(e, 2):
                    dve.wait_ge(s2, e.v - 1)
                dve.scalar_tensor_tensor(hs[:, e.r % 2, :, :].rearrange("p c n -> p (c n)"), th[:, e.r % 2, :], 1.0,
                                         bank[3 + e.r % 2][0:IC, 0:2 * P], ALU.add, ALU.mult).then_inc(hs_done, 1)

            dve.wait_ge(route_done, 1)
            dve.wait_ge(plan_done, 1)
            chunks = [dve.value_load(plan[0:1, NOV + i:NOV + i + 1], min_val=0, max_val=B) for i in range(OVER)]
            experts(dve, [(L_HOT, hot_rows), (L_IDX, indices), (L_S1, hidden)],
                    {"up": shared_hidden, "down": shared_add})
            n_over = dve.value_load(plan[0:1, 2 * NOV:2 * NOV + 1], min_val=0, max_val=NOV)
            for r in range(4):
                dve.wait_ge(y_out[r], 16 * ((TILES - r + 3) // 4))
            with dve.If(n_over > OVER):
                with dve.Fori(0, n_over - OVER) as i:
                    c = dve.value_load(plan[0:1, bass.ds(i + (NOV + OVER), 1)], min_val=1, max_val=7)
                    dve.wait_ge(v_pick, i + 1)
                    dve.tensor_tensor(onehot[:, 0, :, :],
                                      iota_w[:, bass.ds(c * P, P)].rearrange("p (o j) -> p o j", o=1).to_broadcast([P, B, P]),
                                      picked[:, 0, :, 0:1].to_broadcast([P, B, P]), ALU.is_equal).then_inc(v_hot, 1)
                    dve.wait_ge(v_inv, i + 1)
                    dve.wait_ge(v_free, i + 1)
                    src = bank[0][:, 0:3]
                    dve.tensor_copy(g_idx[:, 0:1], src[:, 0:1])
                    dve.tensor_scalar(s_idx[:, 0:1], src[:, 1:2], float(FAR), src[:, 2:3],
                                      ALU.add, ALU.add).then_inc(v_idx, 1)
                    dve.wait_ge(v_th, i + 1)
                    dve.scalar_tensor_tensor(hs[:, 0, :, :].rearrange("p c n -> p (c n)"), th[:, 0, :], 1.0,
                                             bank[3][0:IC, 0:2 * P], ALU.add, ALU.mult).then_inc(v_hs, 1)
            with dve.Else():
                dve.nop()
            for b in range(B):
                if b not in ON_PE:
                    dve.wait_ge(y6_in[b % 4], 16 * (b // 4 + 1))
                    for k in range(K):
                        ins = dve.scalar_tensor_tensor(x_sb[:, b, :], y6[:, b % 4, k, :], ww[:, b, k:k + 1], x_sb[:, b, :],
                                                       ALU.mult, ALU.add)
                        if k < K - 1:
                            link(ins)
                    ins.then_inc(mixed[0], 1)

        @block.tensor
        def _(pe):
            mm = nc.tensor.matmul
            tr = nc.tensor.transpose

            def t_taken(kind, b, c):
                return {"max": (nm_done, 2 * (b + 1)), "out": (on_done, 2 * b + c + 1), "back": (x1_done, b + 1)}[kind]

            pe.wait_ge(consts, 9)
            pe.wait_ge(ld_mask, 32)
            tr(bank[0][:, 0:B * TC], mask_r[:, :], ident[0:B * TC, 0:B * TC]).then_inc(proj, 1)
            pe.wait_ge(ld_ctx, 16)
            pe.wait_ge(ld_w, 48)
            for j in range(B):
                k_side, c = j % 2 == 0, 2 * (j // 2)
                if not k_side:
                    pe.wait_ge(normed, c + 2)
                if j == 7:
                    pe.wait_ge(mask_col, 1)
                src = (ctx_sb if k_side else xn)[:, c:c + 2, :].rearrange("p b t -> p (b t)")
                mm(bank[(j + 1) % 8], w_sb[:, 0 if k_side else 1, :], src, start=True, stop=True).then_inc(proj, 1)
            for j in range(4):
                pe.wait_ge(fulls, j + 1)
                for s in range(4):
                    b, c = divmod(4 * j + s, TC)
                    last = mm(bank[(j + 1) % 8][:, s * P:(s + 1) * P], ctx_sb[:, b, c * P:(c + 1) * P], w_sb[:, 2, :],
                              start=True, stop=True)
                last.then_inc(proj, 1)
            pe.wait_ge(fulls, B)
            pe.wait_ge(taken, 4)

            t_last = None
            for a in range(STEPS):
                if a < NA:
                    b, h = divmod(a, H)
                    if h == 0:
                        pe.wait_ge(stack_in[b % 3], 80 * (b // 3 + 1))
                    if a >= 2:
                        pe.wait_ge(max_done, a - 1)
                    for c in range(TC):
                        last = mm(bank[a % 2][:, c * T:(c + 1) * T], q_st[b % 3][0:AROWS, h, c * P:(c + 1) * P],
                                  k_st[b % 3][0:AROWS, h, :], start=True, stop=True)
                    last.then_inc(a_done, 1)
                p = pair_of(a)
                if p is not None:
                    b, h = divmod(2 * p, H)
                    if h == 0:
                        pe.wait_ge(max_in, 16 * (b + 1))
                        pe.wait_ge(ones_in, 48)
                    if p >= 2:
                        pe.wait_ge(exp_done, p - 1)
                    for i in range(2):
                        for c in range(TC):
                            o = (i * TC + c) * T
                            last = mm(score[p % 2][:, o:o + T], k_st[b % 3][0:BROWS, h + i, c * P:(c + 1) * P],
                                      q_st[b % 3][0:BROWS, h + i, :], start=True, stop=True)
                    last.then_inc(b_done, 1)
                gq = group_of(a)
                if gq is not None:
                    b, g = divmod(gq, 4)
                    pe.wait_ge(exp_done, 2 * gq + 2)
                    if gq >= 1:
                        pe.wait_ge(os_done, gq)
                    if g == 0:
                        pe.wait_ge(v_ready, b + 1)
                    for c in range(TC):
                        for i in range(4):
                            pr = probs[:, (2 * gq + i // 2) % 4, :].rearrange("p (i c t) -> p i c t", i=2, c=TC)
                            last = mm(bank[6][32 * i:32 * i + 32, 0:T], v_pad[:, b % 2, c, 4 * g + i, :],
                                      pr[:, i % 2, c, :], start=(c == 0), stop=(c == TC - 1))
                    last.then_inc(pv_done, 1)
                for kind, b, c in events.get(a, []):
                    if t_last is not None:
                        pe.wait_ge(*t_taken(*t_last))
                    t_last = (kind, b, c)
                    if kind == "max":
                        pe.wait_ge(max_done, 16 * (b + 1))
                        for i in range(TC):
                            last = tr(bank[7][0:H, i * P:(i + 1) * P], mx[:, b % 2, i, :], ident[:, :])
                    elif kind == "out":
                        pe.wait_ge(os_done, 4 * (b + 1))
                        for g in range(4):
                            last = tr(bank[7][:, g * P:(g + 1) * P], o_sb[:, b % 2, g, c * P:(c + 1) * P], ident[:, :])
                    else:
                        pe.wait_ge(on_done, 2 * (b + 1))
                        for i in range(TC):
                            last = tr(bank[7][:, i * P:(i + 1) * P], o_n[:, i, :], ident[:, :])
                    last.then_inc(t_ready, 1)

            for b in range(B):
                pe.wait_ge(tok_normed, b + 1)
                if b >= 2:
                    pe.wait_ge(xt_done, b - 1)
                for k in range(TC):
                    last = tr(bank[b % 2][:, k * P:(k + 1) * P], xn[:, b, k * P:(k + 1) * P], ident[:, :])
                last.then_inc(xt_ready, 1)
            pe.wait_ge(ld_gate, 16)
            pe.wait_ge(exp_done, NP)
            for b in range(B):
                pe.wait_ge(xt_done, b + 1)
                for k in range(TC):
                    last = mm(bank[2][:, b * E:(b + 1) * E], xt[:, k, b * P:(b + 1) * P], gate_sb[:, k, :],
                              start=(k == 0), stop=(k == TC - 1))
            last.then_inc(lg_ready, 1)

            def shared_up(j):
                nb, c = divmod(j, 4)
                if j >= 2:
                    pe.wait_ge(sh_done, j - 1)
                for half in range(2):
                    for k in range(TC):
                        last = mm(bank[3 + 2 * (j % 2) + half][0:IC, :], sgu_sb[:, k, 4 * half + c, :],
                                  xt[:, k, nb * 512:(nb + 1) * 512], start=(k == 0), stop=(k == TC - 1))
                last.then_inc(sg_ready, 1)

            def shared_down(b):
                pe.wait_ge(sh_done, 4 * (b // 4 + 1))
                if b >= 2:
                    pe.wait_ge(acc_done, b - 1)
                for c in range(4):
                    last = mm(bank[1 + b % 2][:, 0:T], s_h[:, c, b * P:(b + 1) * P], sd_sb[:, c, :],
                              start=(c == 0), stop=(c == 3))
                last.then_inc(sdn_ready, 1)
                if b == B - 1:
                    pe.wait_ge(acc_done, B)

            pe.wait_ge(x1_done, B)
            pe.wait_ge(os_done, NG)
            pe.wait_ge(ld_shared, 32)
            for j in range(3):
                shared_up(j)
            pe.wait_ge(chosen_done, 1)
            for b in range(B):
                for b2 in range(b + 1):
                    last = mm(bank[7][:, b * E:(b + 1) * E], (tri if b2 == b else ones16)[:, :], chosen[:, b2, :],
                              start=(b2 == 0), stop=(b2 == b))
            last.then_inc(pos_ready, 1)
            pe.wait_ge(lg_done, 1)
            for b in range(B):
                last = mm(bank[2][0:E, 0:1], chosen[:, b, :], ones16[:, 0:1], start=(b == 0), stop=(b == B - 1))
            last.then_inc(cnt_ready, 1)
            shared_up(3)
            pe.wait_ge(beg_in, 1)
            mm(bank[2][0:E, 8:9], tri_f[:, :], extra[:, :], start=True, stop=True).then_inc(beg_ready, 1)
            shared_up(4)
            pe.wait_ge(plan_in, 1)
            mm(bank[2][0:1, 16:16 + NOV], iota_p[0:E, :], t_in[:, :], start=True, stop=True)
            mm(bank[2][0:1, 16 + NOV:16 + 2 * NOV], ones_f[:, :], t_c2[:, :], start=True, stop=True)
            mm(bank[2][0:1, 16 + 2 * NOV:17 + 2 * NOV], ones_f[:, :], extra[:, :], start=True, stop=True).then_inc(plan_ready, 1)
            pe.wait_ge(plan_done, 1)

            def invert(e):
                pe.wait_ge(hot, e.v + 1)
                if not first(e, 2):
                    pe.wait_ge(idx, e.v - 1)
                for b in range(B):
                    last = mm(bank[7 * (e.r % 2)][:, 0:3], onehot[:, e.r % 2, b, :], picked[:, e.r % 4, b, 1:4],
                              start=(b == 0), stop=(b == B - 1))
                last.then_inc(inv, 1)

            def transpose_rows(e):
                pe.wait_ge(rows_in[e.r % 4], 16 * (e.use(4) + 1))
                if not first(e, 2):
                    pe.wait_ge(xe_done, e.v - 1)
                for k in range(TC):
                    last = tr(bank[1 + e.r % 2][:, k * P:(k + 1) * P], rows[:, e.r % 4, k * P:(k + 1) * P], ident[:, :])
                last.then_inc(xpose, 1)

            def first_product(e):
                pe.wait_ge(w_in[e.r % 4], 32 * (e.use(4) + 1))
                pe.wait_ge(xe_done, e.v + 1)
                if not first(e, 2):
                    pe.wait_ge(hs_done, e.v - 1)
                for c in range(2):
                    for k in range(TC):
                        last = mm(bank[3 + e.r % 2][0:IC, c * P:(c + 1) * P], w1_sb[:, e.r % 4, k, c * IC:(c + 1) * IC],
                                  xe[:, e.r % 2, k, :], start=(k == 0), stop=(k == TC - 1))
                last.then_inc(s1, 1)

            def second_product(e):
                pe.wait_ge(hs_done, e.v + 1)
                if not first(e, 2):
                    pe.wait_ge(y_done, e.v - 1)
                for c in range(2):
                    last = mm(bank[5 + e.r % 2][:, 0:T], hs[:, e.r % 2, c, :], w2_sb[0:IC, e.r % 4, c, :],
                              start=(c == 0), stop=(c == 1))
                last.then_inc(s2, 1)

            experts(pe, [(0, second_product), (L_S1, first_product), (L_X, transpose_rows), (L_INV, invert)],
                    {"up": shared_up, "down": shared_down})
            n_over = pe.value_load(plan[0:1, 2 * NOV:2 * NOV + 1], min_val=0, max_val=NOV)
            pe.wait_ge(y_done, TILES)
            pe.sem_inc(v_s2, 1)
            with pe.If(n_over > OVER):
                with pe.Fori(0, n_over - OVER) as i:
                    pe.wait_ge(v_hot, i + 1)
                    for b in range(B):
                        last = mm(bank[0][:, 0:3], onehot[:, 0, b, :], picked[:, 0, b, 1:4], start=(b == 0), stop=(b == B - 1))
                    last.then_inc(v_inv, 1)
                    pe.wait_ge(v_rows, 16 * i + 16)
                    for k in range(TC):
                        last = tr(bank[1][:, k * P:(k + 1) * P], rows[:, 0, k * P:(k + 1) * P], ident[:, :])
                    last.then_inc(v_x, 1)
                    pe.wait_ge(v_w, 32 * i + 32)
                    pe.wait_ge(v_xe, i + 1)
                    for c in range(2):
                        for k in range(TC):
                            last = mm(bank[3][0:IC, c * P:(c + 1) * P], w1_sb[:, 0, k, c * IC:(c + 1) * IC],
                                      xe[:, 0, k, :], start=(k == 0), stop=(k == TC - 1))
                    last.then_inc(v_s1, 1)
                    pe.wait_ge(v_hs, i + 1)
                    pe.wait_ge(v_free, i + 1)
                    for c in range(2):
                        last = mm(bank[5][:, 0:T], hs[:, 0, c, :], w2_sb[0:IC, 0, c, :], start=(c == 0), stop=(c == 1))
                    last.then_inc(v_s2, 1)
            with pe.Else():
                pe.nop()
            for n, b in enumerate(ON_PE):
                pe.wait_ge(weighted, n + 1)
                if n >= 2:
                    pe.wait_ge(mixed[1], n - 1)
                for k in range(K + 1):
                    last = mm(bank[n % 2][:, 0:T], ident[:, :], y6[:, b % 4, k, :] if k < K else x_sb[:, b, :],
                              start=(k == 0), stop=(k == K))
                last.then_inc(summed, 1)


def kernel(**inputs):
    import numpy as np
    import concourse.bacc as bacc
    from concourse.bass_utils import run_bass_kernel_spmd as run

    P, H, D, IC = 128, 16, 8, 96
    a = {k: np.asarray(v) for k, v in inputs.items()}
    by_width = np.arange(H * D).reshape(H, D).T.reshape(-1)

    def pad(w, axis, size):
        width = [(0, 0)] * w.ndim
        width[axis] = (0, size - w.shape[axis])
        return np.pad(w, width)

    E, I, T = a["L0_ffn_experts_w1"].shape
    half = I // 2
    w1 = pad(a["L0_ffn_experts_w1"].reshape(E, 2, half, T // P, P), 2, IC)
    w2 = pad(a["L0_ffn_experts_w2"].reshape(E, T, 2, half), 3, P)
    sgu = pad(a["L0_ffn_shared_gate_up"].reshape(8, half, T // P, P), 1, IC)
    sd = pad(a["L0_ffn_shared_down"].reshape(T, 4, half), 2, IC)
    laid = {
        "x": a["x"].transpose(1, 0, 2), "ctx": a["ctx_2048"].transpose(1, 0, 2), "mask": a["mask_Bx1x2048_fk1"][:, 0],
        "g_xattn": a["g_xattn"][None], "g_ffn": a["g_ffn"][None],
        "wq": a["L0_xattn_Wq"][by_width].T, "bq": a["L0_xattn_bq"][by_width][:, None],
        "wk": a["L0_xattn_Wk"][by_width].T, "bk": a["L0_xattn_bk"][by_width][:, None],
        "wv": a["L0_xattn_Wv"].T, "bv": a["L0_xattn_bv"][None],
        "gate": a["L0_ffn_gate_w"].T.reshape(T // P, P, E).transpose(1, 0, 2),
        "w1": w1.transpose(0, 4, 3, 1, 2).reshape(E, P, T // P, 2 * IC),
        "w2": w2.transpose(0, 3, 2, 1),
        "sgu": sgu.transpose(3, 2, 0, 1), "sd": sd.transpose(2, 1, 0),
    }
    nc = bacc.Bacc("TRN2", target_bir_lowering=False, num_devices=1)
    arrays, args = {}, []
    for name, w in laid.items():
        w = np.ascontiguousarray(w)
        arrays[f"in_{name}"] = w
        args.append(nc.dram_tensor(f"in_{name}", w.shape, mybir.dt.from_np(w.dtype), kind="ExternalInput").ap())
    out = nc.dram_tensor("out", (P, a["x"].shape[0], T), mybir.dt.float32, kind="ExternalOutput").ap()
    build_gated_block(nc, *args, out)
    r = run(nc, [arrays], core_ids=[0])
    return np.ascontiguousarray(np.asarray(r.results[0]["out"]).transpose(1, 0, 2))
```

```python
import concourse.bass as bass
from concourse import mybir
from contextlib import ExitStack


def build_gated_block(nc, x, ctx_in, mask, g_xattn, g_ffn, wq, bq, wk, bk, wv, bv, gate, w1, w2, sgu, sd, out):
    F32, F32R, F16, U32, I32 = (mybir.dt.float32, mybir.dt.float32r, mybir.dt.float16, mybir.dt.uint32,
                                mybir.dt.int32)
    ALU, ACT, AX = mybir.AluOpType, mybir.ActivationFunctionType, mybir.AxisListType

    P = 128
    B, T = x.shape[1], x.shape[2]
    H, D = 16, 8
    TC = T // P
    E = gate.shape[2]
    K = 6
    OVER = 2
    TILES = E + OVER
    NT = B * P
    IC = sd.shape[0]
    EPS = 1e-5
    NEG = 1000000.0
    ROOT = float(D) ** 0.5
    HD1 = D + 1
    PART = 2 * HD1
    SROWS = 2 * PART
    AROWS = 96
    BROWS = AROWS + 2
    FAR = 8192

    es = ExitStack()
    with es:
        def sb(name, shape, dt=F32):
            return es.enter_context(nc.sbuf_tensor(name, shape, dt))

        def sem(name):
            return es.enter_context(nc.semaphore(name))

        q_parts = nc.dram_tensor("q_parts", [B, 2, HD1 * H, T], F32).ap()
        k_parts = nc.dram_tensor("k_parts", [B, 2, HD1 * H, T], F32).ap()
        tokens = nc.dram_tensor("tokens", [NT, T], F32).ap()
        routed = nc.dram_tensor("routed", [NT * K, T], F32).ap()

        x_sb = sb("x_sb", [P, B, T])
        ctx_sb = sb("ctx_sb", [P, B, T])
        xn = sb("xn", [P, B, T])
        vals = sb("vals", [P, B * TC, P])
        v_pad = sb("v_pad", [P, 2, TC, H, 32])
        probs = sb("probs", [P, 4, 2 * TC * T])
        o_sb = sb("o_sb", [P, 2, 4, T])
        o_n = sb("o_n", [P, TC, P])
        full = sb("full", [P, 2, 2 * T])
        high = sb("high", [P, 2, 2 * T], F32R)
        low = sb("low", [P, 2, 2 * T], F32R)
        w_sb = sb("w_sb", [P, 3, P])
        b_sb = sb("b_sb", [P, 2])
        bv_sb = sb("bv_sb", [P, P])
        mask_bc = sb("mask_bc", [P, B * T])
        mask_r = sb("mask_r", [B * TC, P])
        mask_c = sb("mask_c", [P, B * TC])
        mask_b = sb("mask_b", [B, T])
        mask_k = sb("mask_k", [B, T])
        mask_hl = sb("mask_hl", [B, 4, T], F32R)
        ident = sb("ident", [P, P])
        zeros = sb("zeros", [P, 1])
        ones_st = sb("ones_st", [2, T])
        stats = sb("stats", [P, B, 6])
        mv = sb("mv", [P, B, 2])
        var = sb("var", [P, B])
        rstd = sb("rstd", [P, B])
        neg_half = sb("neg_half", [P, B])
        mx = sb("mx", [P, 2, TC, H])
        nm = sb("nm", [H, 2, 2, T], F32R)
        rz = sb("rz", [P, H])
        g_sb = sb("g_sb", [P, 2])
        tg = sb("tg", [P, 3])
        xt = ctx_sb[:, :, :].rearrange("p b t -> p (b t)").rearrange("p (k n) -> p k n", k=TC)
        gate_sb = sb("gate_sb", [P, TC, E])
        v8 = sb("v8", [P, B, 8])
        i8 = sb("i8", [P, B, 8], U32)
        if8 = sb("if8", [P, B, 8])
        iota_e = sb("iota_e", [P, E])
        route = vals[:, :, :].rearrange("p s n -> p (s n)").bitcast(F16)[:, 0:B * E * 4].rearrange("p (b e n) -> p b e n", b=B, e=E)
        picked = sb("picked", [P, 4, B, 4], F16)
        iota_w = sb("iota_w", [P, NT + P], F16)
        iota_t = sb("iota_t", [P, B])
        iota_p = sb("iota_p", [P, 1])
        low6 = sb("low6", [P, 1])
        tri = sb("tri", [P, P], F16)
        tri_f = sb("tri_f", [E, E])
        ones16 = sb("ones16", [P, P], F16)
        ones_f = sb("ones_f", [E, 1])
        e6 = sb("e6", [P, B, K])
        e6s = sb("e6s", [P, B])
        ww = sb("ww", [P, B, K])
        n_e = sb("n_e", [E, 1])
        c128 = sb("c128", [E, 7])
        c_tmp = sb("c_tmp", [E, 7])
        extra = sb("extra", [E, 1])
        o_beg = sb("o_beg", [E, 1])
        o_end = sb("o_end", [E, 1])
        NOV = NT * K // (P + 1)
        iota_q = sb("iota_q", [E, NOV])
        t_ge = sb("t_ge", [E, NOV])
        t_in = sb("t_in", [E, NOV])
        t_c = sb("t_c", [E, NOV])
        t_c2 = sb("t_c2", [E, NOV])
        plan = sb("plan", [1, 2 * NOV + 1], I32)

        g_idx = sb("g_idx", [P, 8], U32)
        s_idx = sb("s_idx", [P, 8], U32)

        with ExitStack() as attention:
            q_st, k_st = [None] * 3, [None] * 3
            for n in (2, 0, 1):
                for name, st in (("q_st", q_st), ("k_st", k_st)):
                    st[n] = attention.enter_context(nc.sbuf_tensor(f"{name}{n}", [P, H, T], F32R))
        with ExitStack() as shared:
            def shared_sb(name, shape):
                return shared.enter_context(nc.sbuf_tensor(name, shape, F32))

            sgu_sb = shared_sb("sgu_sb", [P, TC, 8, IC])
            sd_sb = shared_sb("sd_sb", [IC, 4, T])
            s_h = shared_sb("s_h", [IC, 4, NT])
            s_th = shared_sb("s_th", [IC, 2, 512])
        y6 = sb("y6", [P, B, K, T])
        w1_sb = sb("w1_sb", [P, 4, TC, 2 * IC])
        w2_sb = sb("w2_sb", [IC, 4, 2, T])
        onehot = sb("onehot", [P, 2, B, P], F16)
        rows = sb("rows", [P, 4, T])
        xe = sb("xe", [P, 2, TC, P])
        th = sb("th", [IC, 2, 2 * P])
        hs = sb("hs", [IC, 2, 2, P])
        y_sb = sb("y_sb", [P, 4, T])
        far = full[:, 1, :].rearrange("p (b e) -> p b e", b=B)
        eq = mask_bc[:, 0:K * E].rearrange("p (k e) -> p k e", k=K)
        chosen = mask_bc[:, 512:512 + B * E // 2].bitcast(F16).rearrange("p (b e) -> p b e", b=B)
        s_gg = mask_bc[0:IC, 1024:2048].rearrange("p (r n) -> p r n", r=2)

        def ps(name, banks):
            return es.enter_context(nc.psum_tensor(name, [P, 512 * banks], F32))

        b0, b1 = ps("b0", 1), ps("b1", 1)
        score = [ps("score0", 2), ps("score1", 2)]
        b6, b7 = ps("b6", 1), ps("b7", 1)
        bank = [b0[:, :], b1[:, :], score[0][:, 0:512], score[0][:, 512:1024], score[1][:, 0:512],
                score[1][:, 512:1024], b6[:, :], b7[:, :]]

        ld_x, ld_ctx, ld_w, ld_small, ld_mask, ld_bc, ld_gate, ld_shared = [sem(n) for n in (
            "ld_x", "ld_ctx", "ld_w", "ld_small", "ld_mask", "ld_bc", "ld_gate", "ld_shared")]
        consts = sem("consts")
        zeroed = [sem(f"zeroed{n}") for n in range(3)]
        zero_col = sem("zero_col")
        ones_done = sem("ones_done")
        ones_in = sem("ones_in")
        dv = sem("dv")
        pl = sem("pl")
        pool_steps = sem("pool_steps")
        var_done, rstd_done, normed = sem("var_done"), sem("rstd_done"), sem("normed")
        proj = sem("proj")
        taken = sem("taken")
        mask_turned = sem("mask_turned")
        mask_col = sem("mask_col")
        aug, aug_out = sem("aug"), sem("aug_out")
        fulls, highs, lows = sem("fulls"), sem("highs"), sem("lows")
        parts_out = [sem(f"parts_out{n}") for n in range(B)]
        stack_in = [sem(f"stack_in{n}") for n in range(3)]
        max_in = sem("max_in")
        a_done, max_done, b_done, exp_done, pv_done, os_done, t_ready, nm_done, v_ready, on_done, x1_done = [
            sem(n) for n in ("a_done", "max_done", "b_done", "exp_done", "pv_done", "os_done", "t_ready",
                             "nm_done", "v_ready", "on_done", "x1_done")]
        tanh_g = sem("tanh_g")
        var2_done, rstd2_done, top_done, far_done = [sem(n) for n in ("var2_done", "rstd2_done", "top_done", "far_done")]
        tok_normed, tok_out, xt_done = [sem(n) for n in (
            "tok_normed", "tok_out", "xt_done")]
        soft, softd, chosen_done, pos_ready, cnt_ready, beg_in, beg_ready, plan_in, plan_ready, plan_done, route_done = [
            sem(n) for n in ("soft", "softd", "chosen_done", "pos_ready", "cnt_ready", "beg_in", "beg_ready",
                             "plan_in", "plan_ready", "plan_done", "route_done")]
        sg_ready, sth_done, sh_done, sdn_ready, acc_done = [sem(n) for n in (
            "sg_ready", "sth_done", "sh_done", "sdn_ready", "acc_done")]
        pick_done, hot, inv, idx, xpose, xe_done, s1, th_done, hs_done, s2, y_done = [sem(n) for n in (
            "pick_done", "hot", "inv", "idx", "xpose", "xe_done", "s1", "th_done", "hs_done", "s2", "y_done")]
        w_in = [sem(f"w_in{n}") for n in range(4)]
        rows_in = [sem(f"rows_in{n}") for n in range(4)]
        y_out = [sem(f"y_out{n}") for n in range(4)]
        (v_w, v_pick, v_hot, v_inv, v_idx, v_rows, v_x, v_xe, v_s1, v_th, v_hs, v_s2, v_y, v_out, v_free) = [
            sem(f"over_{n}") for n in ("w", "pick", "hot", "inv", "idx", "rows", "x", "xe", "s1", "th", "hs", "s2", "y", "out",
                                       "free")]
        y6_in = [sem(f"y6_in{n}") for n in range(B)]
        scattered, stored = sem("scattered"), sem("stored")
        mixed = [sem("mixed_dve"), sem("mixed_act")]
        weights_done, weighted, summed = sem("weights_done"), sem("weighted"), sem("summed")

        block = es.enter_context(nc.Block())

        NA = B * H
        LAG = 24
        BACK = LAG + 27
        NP = NA // 2
        NG = NA // 4

        def pair_at(a):
            return (a - LAG) // 2 if a >= LAG and (a - LAG) % 2 == 0 else -1

        def pair_of(a):
            p = pair_at(a)
            return p if 0 <= p < NP else None

        def group_of(a):
            p = pair_at(a)
            return (p - 3) // 2 if p >= 3 and p % 2 == 1 and (p - 3) // 2 < NG else None

        events = {}
        for b in range(B):
            events.setdefault(16 * b + 17, []).append(("max", b, 0))
            events.setdefault(16 * b + LAG + 21, []).append(("out", b, 0))
            events.setdefault(16 * b + LAG + 23, []).append(("out", b, 1))
            events.setdefault(16 * b + BACK, []).append(("back", b, 0))
            events.setdefault(16 * b + BACK + 5, []).append(("tokens", b, 0))
            events.setdefault(16 * b + BACK + 7, []).append(("router", b, 0))
        STEPS = 16 * (B - 1) + BACK + 8
        ZERO_AT = 3
        FULLS, VALUES = 6, 3
        fulls_at = {1 + 2 * n: FULLS + n for n in range(B - FULLS)}
        values_at = {4 + 2 * n: VALUES + n for n in range(4 - VALUES)}
        up_at = {NA + 4 + 8 * j: j for j in range(4)}
        DOWNS = STEPS - 8
        t_index = {e: n for n, e in enumerate(e for a in sorted(events) for e in events[a])}

        L_PICK, L_HOT, L_INV, L_IDX, L_GATHER, L_X, L_S1 = 8, 7, 7, 6, 5, 3, 2
        U = 8
        LOOP = range(1, (E - L_PICK) // U)

        class Ex:

            def __init__(self, q, r):
                self.q, self.r = q + r // U if r >= U or r < 0 else q, r % U
                self.v = self.q * U + self.r

            def use(self, ring):
                return self.q * (U // ring) + self.r // ring

        between = {-8: (("extra", 0), ("up", 5), ("begins", 0)),
                   -7: (("use", 4), ("spans", 0), ("up", 6), ("use", 5), ("plan", 0)),
                   -6: (("take", 0), ("up", 7), ("use", 6), ("load", 0)),
                   -5: (("down", 2), ("down", 3), ("use", 7), ("down", 4), ("down", 5), ("add", 2), ("add", 3), ("add", 4)),
                   -4: (("down", 6), ("down", 7), ("add", 5), ("add", 6), ("add", 7))}

        def experts(eng, stages, others={}):
            def step(q, r, check):
                for lead, f in stages:
                    e = Ex(q, r + lead)
                    if not check or 0 <= e.v < TILES:
                        f(e)

            for n in range(-L_PICK, U):
                step(0, n, True)
                for kind, j in between.get(n, ()):
                    if kind in others:
                        others[kind](j)
            with eng.Fori(LOOP.start, LOOP.stop) as q:
                for r in range(U):
                    step(q, r, False)
            for n in range(U * LOOP.stop, TILES):
                step(0, n, True)

        def up_bank(j):
            return 0 if j < 4 else 3 + 2 * (j % 2)

        def down_bank(b):
            return b if b < 2 else 1 + b % 2

        def expert_of(e, over):
            return over[e.v - E] if isinstance(e.v, int) and e.v >= E else e.v

        def first(e, n):
            return isinstance(e.v, int) and e.v < n

        ON_PE = (1, 3, 5)

        def mixed_by(b):
            side = b in ON_PE
            return mixed[side], sum((b2 in ON_PE) == side for b2 in range(b + 1))

        def ranks(eng, link, b):
            eng.wait_ge(top_done, b + 1)
            link(eng.tensor_copy(if8[:, b, :], i8[:, b, :]))
            for k in range(K):
                last = eng.tensor_scalar(eq[:, k, :], iota_e[:, :], if8[:, b, k:k + 1], float(k + 1),
                                          ALU.is_equal, ALU.mult)
            link(last)
            link(eng.tensor_tensor(eq[:, 0:3, :], eq[:, 0:3, :], eq[:, 3:6, :], ALU.add))
            link(eng.tensor_tensor(eq[:, 0, :], eq[:, 0, :], eq[:, 1, :], ALU.add))
            rank = eq[:, 0, :]
            link(eng.tensor_tensor(rank, rank, eq[:, 2, :], ALU.add))
            eng.tensor_scalar(chosen[:, b, :], rank, 1.0, None, ALU.min).then_inc(chosen_done, 1)
            eng.tensor_scalar(route[:, b, :, 3], rank, low6[:, 0:1], None, ALU.add)
            eng.tensor_scalar(route[:, b, :, 1], iota_e[:, :], 0.0, iota_t[:, b:b + 1], ALU.mult, ALU.add)
            eng.memset(route[:, b, :, 2], float(K * P * b - FAR))
            link(eng.tensor_scalar(far[:, b, :], rank, 1.0, None, ALU.min))
            eng.tensor_scalar(far[:, b, :], far[:, b, :], float(FAR), -float(FAR), ALU.mult, ALU.add).then_inc(far_done, 1)

        @block.sync
        def _(sp):
            sp.dma_start(x_sb[:, :, :], x).then_inc(ld_x, 16)
            for n, w in enumerate((wk, wq, wv)):
                sp.dma_start(w_sb[:, n, :], w).then_inc(ld_w, 16)
            sp.dma_start(ctx_sb[:, :, :], ctx_in).then_inc(ld_ctx, 16)
            sp.dma_start(mask_bc[:, :], mask.rearrange("(o b) t -> o (b t)", o=1).to_broadcast([P, B * T])).then_inc(ld_bc, 16)
            sp.dma_start(gate_sb[:, :, :], gate).then_inc(ld_gate, 16)
            sp.wait_ge(aug, 4)
            for parts, m in ((q_parts, 0), (k_parts, 2)):
                for hl in range(2):
                    dst = parts[:, hl, D * H:HD1 * H, :]
                    sp.dma_start(dst, mask_hl[:, m + hl:m + hl + 1, :].bitcast(F32).to_broadcast([B, H, T])).then_inc(aug_out, 16)
            sp.wait_ge(ones_done, 1)
            for s in range(3):
                sp.dma_start(k_st[s][AROWS:BROWS, :, :].bitcast(F32),
                             ones_st[:, :].rearrange("p (o t) -> p o t", o=1).to_broadcast([2, H, T])).then_inc(ones_in, 16)

            def send_parts(j):
                parts, n = (q_parts if j % 2 else k_parts), j // 2
                for hl, (t, done) in enumerate(((high, highs), (low, lows))):
                    sp.wait_ge(done, j + 1)
                    dst = parts[2 * n:2 * n + 2, hl, 0:D * H, :].rearrange("b p t -> p b t")
                    sp.dma_start(dst, t[:, j % 2, :].bitcast(F32).rearrange("p (b t) -> p b t", b=2)).then_inc(parts_out[j], 16)

            def load_stacks(b):
                s, use = b % 3, stack_in[b % 3]
                sp.wait_ge(parts_out[b // 2 * 2], 32)
                sp.wait_ge(parts_out[b // 2 * 2 + 1], 32)
                if b == 0:
                    sp.wait_ge(aug_out, 64)
                if b < 3:
                    sp.wait_ge(zeroed[b], 2)
                if b >= 3:
                    sp.wait_ge(b_done, 8 * (b - 2))
                qp = q_parts[b].rearrange("l (d h) t -> (l d) (h t)", h=H)
                kp = k_parts[b].rearrange("l (d h) t -> (l d) (h t)", h=H)
                flatq = q_st[s][:, :, :].bitcast(F32).rearrange("p h t -> p (h t)")
                flatk = k_st[s][:, :, :].bitcast(F32).rearrange("p h t -> p (h t)")
                sp.dma_start(flatq[0:PART, :], qp).then_inc(use, 16)
                sp.dma_start(flatq[PART:SROWS, :], qp).then_inc(use, 16)
                sp.dma_start(flatk[0:PART, :], kp).then_inc(use, 16)
                sp.dma_start(flatk[PART:PART + HD1, :], kp[HD1:PART, :]).then_inc(use, 16)
                sp.dma_start(flatk[PART + HD1:SROWS, :], kp[0:HD1, :]).then_inc(use, 16)

            def send_max(b):
                sp.wait_ge(nm_done, 2 * (b + 1))
                for hl in range(2):
                    sp.dma_start(q_st[b % 3][AROWS + hl:AROWS + hl + 1, :, :].bitcast(F32),
                                 nm[:, b % 2, hl, :].bitcast(F32)).then_inc(max_in, 16)

            def send_tokens(b):
                sp.wait_ge(tok_normed, b + 1)
                sp.dma_start(tokens[b * P:(b + 1) * P, :], xn[:, b, :]).then_inc(tok_out, 16)

            for j in range(B):
                send_parts(j)
                if j in (2, 5, 7):
                    load_stacks((2, 5, 7).index(j))
            for b in range(B):
                if b == B - 1:
                    sp.wait_ge(b_done, 8 * 6)
                    sp.dma_start(sgu_sb[:, :, :, :], sgu).then_inc(ld_shared, 16)
                    sp.dma_start(sd_sb[:, :, :], sd).then_inc(ld_shared, 16)
                send_max(b)
                if 1 <= b and b + 2 < B:
                    load_stacks(b + 2)
                if b >= 3:
                    send_tokens(b - 3)
            for b in range(B - 3, B - 1):
                send_tokens(b)

            over = ()

            def load_weights(e):
                r = e.r % 4
                if not first(e, 4):
                    sp.wait_ge(s2, e.v - 3)
                sp.dma_start(w1_sb[:, r, :, :], w1[bass.ds(expert_of(e, over), 1)].rearrange("o p k i -> p (o k) i")).then_inc(w_in[r], 16)
                sp.dma_start(w2_sb[:, r, :, :], w2[bass.ds(expert_of(e, over), 1)].rearrange("o p c t -> p (o c) t")).then_inc(w_in[r], 16)

            sp.wait_ge(b_done, NP)
            for e in range(3):
                load_weights(Ex(0, e))
            send_tokens(B - 1)

            def load_later(e):
                if not first(e, 3):
                    load_weights(e)

            sp.wait_ge(plan_done, 1)
            over = [sp.value_load(plan[0:1, i:i + 1], min_val=0, max_val=E - 1) for i in range(OVER)]
            experts(sp, [(3, load_later)])
            n_over = sp.value_load(plan[0:1, 2 * NOV:2 * NOV + 1], min_val=0, max_val=NOV)
            sp.wait_ge(s2, TILES)
            with sp.If(n_over > OVER):
                with sp.Fori(0, n_over - OVER) as i:
                    e = sp.value_load(plan[0:1, bass.ds(i + OVER, 1)], min_val=0, max_val=E - 1)
                    sp.wait_ge(v_s2, i + 1)
                    sp.dma_start(w1_sb[:, 0, :, :], w1[bass.ds(e, 1)].rearrange("o p k i -> p (o k) i")).then_inc(v_w, 16)
                    sp.dma_start(w2_sb[:, 0, :, :], w2[bass.ds(e, 1)].rearrange("o p c t -> p (o c) t")).then_inc(v_w, 16)
            with sp.Else():
                sp.nop()
            sp.wait_ge(scattered, 1)
            for b in range(B):
                src = routed[b * P * K:(b + 1) * P * K, :].rearrange("(p k) t -> p k t", k=K)
                sp.dma_start(y6[:, b, :, :], src).then_inc(y6_in[b], 16)
            for b in range(B):
                sp.wait_ge(*mixed_by(b))
                sp.dma_start(out[:, b, :], x_sb[:, b, :]).then_inc(stored, 16)
            sp.wait_ge(stored, 16 * B)

        @block.gpsimd
        def _(pool):
            n = [0]

            def link(ins):
                n[0] += 1
                ins.then_inc(pl, 1)
                pool.wait_ge(pl, n[0])

            pool.memset(zeros[:], 0.0).then_inc(zero_col, 1)
            pool.memset(ones_st[:], 1.0).then_inc(ones_done, 1)
            pool.memset(k_st[0][0:AROWS, :, :].bitcast(F32), 0.0).then_inc(zeroed[0], 1)
            link(pool.memset(ident[:], 0.0))
            link(pool.affine_select(out=ident[:], in_=ident[:], compare_op=ALU.not_equal, fill=1.0, base=0,
                                    pattern=[[-1, P]], channel_multiplier=1))
            pool.memset(ones16[:], 1.0).then_inc(consts, 1)
            link(pool.memset(tri[:], 1.0))
            link(pool.affine_select(out=tri[:], in_=tri[:], compare_op=ALU.is_gt, fill=0.0, base=0,
                                    pattern=[[1, P]], channel_multiplier=-1))
            link(pool.memset(tri_f[:], 1.0))
            link(pool.affine_select(out=tri_f[:], in_=tri_f[:], compare_op=ALU.is_gt, fill=0.0, base=0,
                                    pattern=[[1, E]], channel_multiplier=-1))
            link(pool.memset(ones_f[:], 1.0))
            link(pool.memset(neg_half[:], -0.5))
            link(pool.memset(v_pad[:, :, :, :, :], 0.0))
            link(pool.memset(v_pad[:, :, :, :, D:D + 1], 1.0))
            pool.iota(iota_e[:], pattern=[[1, E]], base=0, channel_multiplier=0, allow_small_or_imprecise_dtypes=True).then_inc(consts, 1)
            pool.iota(iota_w[:], pattern=[[1, NT + P]], base=0, channel_multiplier=0, allow_small_or_imprecise_dtypes=True).then_inc(consts, 1)
            pool.iota(iota_t[:], pattern=[[P, B]], base=0, channel_multiplier=1, allow_small_or_imprecise_dtypes=True).then_inc(consts, 1)
            pool.iota(iota_p[:], pattern=[[0, 1]], base=0, channel_multiplier=1, allow_small_or_imprecise_dtypes=True).then_inc(consts, 1)
            pool.iota(low6[:], pattern=[[0, 1]], base=-1, channel_multiplier=K, allow_small_or_imprecise_dtypes=True).then_inc(consts, 1)
            pool.iota(c128[:], pattern=[[P, 7]], base=P, channel_multiplier=0, allow_small_or_imprecise_dtypes=True).then_inc(consts, 1)
            pool.iota(iota_q[:], pattern=[[1, NOV]], base=0, channel_multiplier=0, allow_small_or_imprecise_dtypes=True).then_inc(consts, 1)
            pool.wait_ge(consts, 8)
            pool.sem_inc(consts, 1)

            pool.wait_ge(var_done, 1)
            pool.tensor_tensor(rstd[:, :], var[:, :], neg_half[:, :], ALU.pow).then_inc(rstd_done, 1)

            for j in range(B):
                pool.wait_ge(highs, j + 1)
                if j >= 2:
                    m = j - 2
                    pool.wait_ge(parts_out[m], 32)
                pool.tensor_tensor(low[:, j % 2, :], full[:, j % 2, :], high[:, j % 2, :].bitcast(F32), ALU.subtract).then_inc(lows, 1)

            for st in (q_st[2], k_st[2]):
                pool.memset(st[0:AROWS, :, :].bitcast(F32), 0.0).then_inc(zeroed[2], 1)

            def values(b):
                if b >= 2:
                    pool.wait_ge(pv_done, 4 * (b - 1))
                for s in range(TC):
                    last = pool.tensor_scalar(v_pad[:, b % 2, s, :, 0:D],
                                              vals[:, b * TC + s, :].rearrange("p (h d) -> p h d", d=D),
                                              mask_c[:, b * TC + s:b * TC + s + 1], None, ALU.mult)
                last.then_inc(v_ready, 1)

            pool.wait_ge(taken, 4)
            pool.wait_ge(mask_col, 1)
            for b in range(3):
                values(b)
            for b in range(B):
                pool.wait_ge(var2_done, b + 1)
                pool.tensor_tensor(rstd[:, b:b + 1], var[:, b:b + 1], neg_half[:, b:b + 1], ALU.pow).then_inc(rstd2_done, 1)
                if b + 3 < B:
                    values(b + 3)
                if b < B - 1:
                    ranks(pool, link, b)
            pool.wait_ge(tok_out, 16 * B)

            def gather(e):
                pool.wait_ge(idx, e.v + 1)
                if not first(e, 4):
                    pool.wait_ge(xpose, e.v - 3)
                pool.sem_inc(pool_steps, 1)
                pool.indirect_dma_start(
                    out=rows[:, e.r % 4, :], out_offset=None, in_=tokens,
                    in_offset=bass.IndirectOffsetOnAxis(ap=g_idx[:, e.r:e.r + 1], axis=0)).then_inc(rows_in[e.r % 4], 16)

            def scatter(e):
                pool.wait_ge(y_done, e.v + 1)
                pool.sem_inc(pool_steps, 1)
                pool.indirect_dma_start(
                    out=routed, out_offset=bass.IndirectOffsetOnAxis(ap=s_idx[:, e.r:e.r + 1], axis=0),
                    in_=y_sb[:, e.r % 4, :], in_offset=None, bounds_check=NT * K - 1,
                    oob_is_err=False).then_inc(y_out[e.r % 4], 16)

            experts(pool, [(0, scatter), (L_GATHER, gather)])
            pool.wait_ge(plan_done, 1)
            n_over = pool.value_load(plan[0:1, 2 * NOV:2 * NOV + 1], min_val=0, max_val=NOV)
            for r in range(4):
                pool.wait_ge(y_out[r], 16 * ((TILES - r + 3) // 4))
            pool.sem_inc(v_free, 1)
            with pool.If(n_over > OVER):
                with pool.Fori(0, n_over - OVER) as i:
                    pool.wait_ge(v_idx, i + 1)
                    pool.sem_inc(pool_steps, 1)
                    pool.indirect_dma_start(
                        out=rows[:, 0, :], out_offset=None, in_=tokens,
                        in_offset=bass.IndirectOffsetOnAxis(ap=g_idx[:, 0:1], axis=0)).then_inc(v_rows, 16)
                    pool.wait_ge(v_y, i + 1)
                    pool.sem_inc(pool_steps, 1)
                    pool.indirect_dma_start(
                        out=routed, out_offset=bass.IndirectOffsetOnAxis(ap=s_idx[:, 0:1], axis=0),
                        in_=y_sb[:, 0, :], in_offset=None, bounds_check=NT * K - 1,
                        oob_is_err=False).then_inc(v_out, 16)
                    pool.wait_ge(v_out, 16 * i + 16)
                    pool.sem_inc(v_free, 1)
            with pool.Else():
                pool.nop()
            pool.sem_inc(scattered, 1)

        @block.scalar
        def _(act):
            act.dma_start(mask_r[:, :], mask.rearrange("b (s p) -> (b s) p", p=P)).then_inc(ld_mask, 16)
            act.dma_start(mask_b[:, :], mask).then_inc(ld_mask, 16)
            act.dma_start(b_sb[:, 0:1], bk).then_inc(ld_small, 16)
            act.dma_start(b_sb[:, 1:2], bq).then_inc(ld_small, 16)
            act.dma_start(bv_sb[:, :], bv.to_broadcast([P, P])).then_inc(ld_small, 16)
            act.dma_start(g_sb[:, 0:1], g_xattn.to_broadcast([P, 1])).then_inc(ld_small, 16)
            act.dma_start(g_sb[:, 1:2], g_ffn.to_broadcast([P, 1])).then_inc(ld_small, 16)
            act.wait_ge(zero_col, 1)

            def zero_rows(st):
                act.activation(st[0:AROWS, :, :].rearrange("p h t -> p (h t)"),
                               zeros[0:AROWS, :].to_broadcast([AROWS, H * T]), ACT.Copy).then_inc(zeroed[1], 1)

            zero_rows(q_st[1])
            act.wait_ge(ld_small, 80)
            act.activation(tg[:, 0:2], g_sb[:, :], ACT.Tanh).then_inc(tanh_g, 1)
            for j in range(B):
                act.wait_ge(fulls, j + 1)
                if j >= 2:
                    act.wait_ge(parts_out[j - 2], 32)
                act.activation(high[:, j % 2, :], full[:, j % 2, :], ACT.Copy).then_inc(highs, 1)
                if j == ZERO_AT:
                    zero_rows(k_st[1])

            def shared_tanh(j):
                act.wait_ge(sg_ready, j + 1)
                if j >= 2:
                    act.wait_ge(sh_done, j - 1)
                act.activation(s_th[:, j % 2, :], bank[up_bank(j)][0:IC, :], ACT.Tanh, scale=0.5).then_inc(sth_done, 1)

            for a in range(STEPS + 2):
                for kind, b, c in events.get(a - 1, []):
                    if kind == "max":
                        act.wait_ge(t_ready, t_index[(kind, b, c)] + 1)
                        if b >= 2:
                            act.wait_ge(max_in, 32 * (b - 1))
                        act.activation(nm[:, b % 2, 0, :], bank[7][0:H, 0:T], ACT.Copy, scale=-1.0).then_inc(nm_done, 1)
                    if kind == "tokens":
                        act.wait_ge(t_ready, t_index[(kind, b, c)] + 1)
                        act.activation(xt[:, :, b * P:(b + 1) * P], bank[7][:, 0:TC * P].rearrange("p (k n) -> p k n", k=TC),
                                       ACT.Copy).then_inc(xt_done, 1)
                gq = group_of(a - TC)
                if gq is not None:
                    b, g = divmod(gq, 4)
                    act.wait_ge(pv_done, gq + 1)
                    if b >= 2 and g == 0:
                        act.wait_ge(x1_done, b - 1)
                    act.activation(o_sb[:, b % 2, g, :], bank[6][:, 0:T], ACT.Copy).then_inc(os_done, 1)
                p = pair_of(a)
                if p is not None:
                    act.wait_ge(b_done, p + 1)
                    if p >= 4:
                        act.wait_ge(pv_done, (p - 4) // 2 + 1)
                    act.activation(probs[:, p % 4, 0:1024], score[p % 2][:, :], ACT.Exp, scale=1.0 / ROOT).then_inc(exp_done, 1)
                if a - 2 in up_at:
                    shared_tanh(up_at[a - 2])

            act.wait_ge(soft, 1)
            act.activation(e6[:, :, :], e6[:, :, :], ACT.Exp).then_inc(softd, 1)


            def pick(e):
                if not first(e, 4):
                    act.wait_ge(inv, e.v - 3)
                act.activation(picked[:, e.r % 4, :, :], route[:, :, bass.ds(expert_of(e, over), 1), :].rearrange("p b o n -> p b (o n)"),
                               ACT.Copy).then_inc(pick_done, 1)

            def take_x(e):
                act.wait_ge(xpose, e.v + 1)
                if not first(e, 2):
                    act.wait_ge(s1, e.v - 1)
                act.activation(xe[:, e.r % 2, :, :], bank[1 + e.r % 2][:, 0:TC * P].rearrange("p (k n) -> p k n", k=TC),
                               ACT.Copy).then_inc(xe_done, 1)

            def tanh(e):
                act.wait_ge(s1, e.v + 1)
                if not first(e, 2):
                    act.wait_ge(hs_done, e.v - 1)
                act.activation(th[:, e.r % 2, :], bank[3 + e.r % 2][0:IC, 0:2 * P], ACT.Tanh, scale=0.5).then_inc(th_done, 1)

            def take_y(e):
                act.wait_ge(s2, e.v + 1)
                if not first(e, 4):
                    act.wait_ge(y_out[e.r % 4], 16 * e.use(4))
                act.activation(y_sb[:, e.r % 4, :], bank[5 + e.r % 2][:, 0:T], ACT.Copy).then_inc(y_done, 1)

            def take_sum(n):
                act.wait_ge(summed, n + 1)
                act.activation(x_sb[:, ON_PE[n], :], bank[n % 2][:, 0:T], ACT.Copy).then_inc(mixed[1], 1)

            act.wait_ge(route_done, 1)
            over = []

            def load_plan(_):
                act.wait_ge(plan_done, 1)
                over.extend(act.value_load(plan[0:1, i:i + 1], min_val=0, max_val=E - 1) for i in range(OVER))

            experts(act, [(L_PICK, pick), (0, take_y), (L_S1, tanh), (L_X, take_x)],
                    {"use": shared_tanh, "load": load_plan})
            act.wait_ge(plan_done, 1)
            n_over = act.value_load(plan[0:1, 2 * NOV:2 * NOV + 1], min_val=0, max_val=NOV)
            for r in range(4):
                act.wait_ge(y_out[r], 16 * ((TILES - r + 3) // 4))
            with act.If(n_over > OVER):
                with act.Fori(0, n_over - OVER) as i:
                    e = act.value_load(plan[0:1, bass.ds(i + OVER, 1)], min_val=0, max_val=E - 1)
                    act.activation(picked[:, 0, :, :], route[:, :, bass.ds(e, 1), :].rearrange("p b o n -> p b (o n)"),
                                   ACT.Copy).then_inc(v_pick, 1)
                    act.wait_ge(v_x, i + 1)
                    act.activation(xe[:, 0, :, :], bank[1][:, 0:TC * P].rearrange("p (k n) -> p k n", k=TC),
                                   ACT.Copy).then_inc(v_xe, 1)
                    act.wait_ge(v_s1, i + 1)
                    act.activation(th[:, 0, :], bank[3][0:IC, 0:2 * P], ACT.Tanh, scale=0.5).then_inc(v_th, 1)
                    act.wait_ge(v_s2, i + 2)
                    act.wait_ge(v_free, i + 1)
                    act.activation(y_sb[:, 0, :], bank[5][:, 0:T], ACT.Copy).then_inc(v_y, 1)
            with act.Else():
                act.nop()
            act.wait_ge(weights_done, 1)
            for n, b in enumerate(ON_PE):
                act.wait_ge(y6_in[b], 16)
                for k in range(K):
                    last = act.activation(y6[:, b, k, :], y6[:, b, k, :], ACT.Copy, scale=ww[:, b, k:k + 1])
                last.then_inc(weighted, 1)
                if n:
                    take_sum(n - 1)
            take_sum(len(ON_PE) - 1)

        @block.vector
        def _(dve):
            n = [0]

            def link(ins):
                n[0] += 1
                ins.then_inc(dv, 1)
                dve.wait_ge(dv, n[0])

            dve.memset(q_st[0][0:AROWS, :, :].bitcast(F32), 0.0).then_inc(zeroed[0], 1)
            dve.wait_ge(ld_mask, 32)
            link(dve.tensor_scalar(mask_k[:, :], mask_b[:, :], NEG * ROOT, -NEG * ROOT, ALU.mult, ALU.add))
            for m, src in enumerate((mask_b, mask_k)):
                dve.tensor_copy(mask_hl[:, 2 * m, :], src[:, :]).then_inc(aug, 1)
                dve.wait_ge(aug, 2 * m + 1)
                dve.tensor_tensor(mask_hl[:, 2 * m + 1, :], src[:, :], mask_hl[:, 2 * m, :].bitcast(F32), ALU.subtract).then_inc(aug, 1)
            def variances():
                for b in range(B):
                    last = dve.bn_stats(stats[:, b, :], x_sb[:, b, :])
                link(last)
                for b in range(B):
                    last = dve.bn_aggr(mv[:, b, :], stats[:, b, :])
                link(last)
                dve.tensor_scalar(var[:, :], mv[:, :, 1], EPS, None, ALU.add).then_inc(var_done, 1)

            def normalize(bs, done):
                for b in bs:
                    dve.tensor_scalar(xn[:, b, :], x_sb[:, b, :], mv[:, b, 0:1], rstd[:, b:b + 1],
                                      ALU.subtract, ALU.mult).then_inc(done, 1)

            dve.wait_ge(ld_x, 16)
            variances()
            dve.wait_ge(ld_small, 80)
            dve.wait_ge(ld_bc, 16)
            def take_projection(j):
                dve.wait_ge(proj, j + 1)
                if j >= 2:
                    dve.wait_ge(lows, j - 1)
                c = (j // 2) * 2 * T
                dve.scalar_tensor_tensor(full[:, j % 2, :], bank[j], b_sb[:, j % 2:j % 2 + 1],
                                         mask_bc[:, c:c + 2 * T], ALU.add, ALU.mult).then_inc(fulls, 1)

            def take_values(j):
                dve.wait_ge(proj, 9 + j)
                dve.tensor_tensor(vals[:, 4 * j:4 * j + 4, :], bank[j + 2].rearrange("p (s n) -> p s n", s=4),
                                  bv_sb[:, :].rearrange("p (o n) -> p o n", o=1).to_broadcast([P, 4, P]), ALU.add).then_inc(taken, 1)

            take_projection(0)
            dve.wait_ge(rstd_done, 1)
            normalize(range(2), normed)
            dve.wait_ge(mask_turned, 1)
            dve.tensor_copy(mask_c[:, :], bank[7][:, 0:B * TC]).then_inc(mask_col, 1)
            take_projection(1)
            normalize(range(2, B), normed)
            for j in range(2, FULLS):
                take_projection(j)
            for j in range(VALUES):
                take_values(j)
            dve.wait_ge(tanh_g, 1)
            dve.wait_ge(mask_col, 1)

            dve.tensor_scalar(tg[:, 2:3], tg[:, 1:2], 0.5, None, ALU.mult)

            def shared_hidden(j):
                g_ps, u_ps = bank[up_bank(j)][0:IC, :], bank[up_bank(j) + 1][0:IC, :]
                nb, c = divmod(j, 4)
                dve.wait_ge(sth_done, j + 1)
                link(dve.scalar_tensor_tensor(s_gg[:, j % 2, :], s_th[:, j % 2, :], 1.0, g_ps, ALU.add, ALU.mult))
                dve.tensor_tensor(s_h[:, c, nb * 512:(nb + 1) * 512], s_gg[:, j % 2, :], u_ps, ALU.mult).then_inc(sh_done, 1)

            def shared_add(b):
                dve.wait_ge(sdn_ready, b + 1)
                dve.scalar_tensor_tensor(x_sb[:, b, :], bank[down_bank(b)][:, 0:T], tg[:, 2:3], x_sb[:, b, :],
                                         ALU.mult, ALU.add).then_inc(acc_done, 1)

            for a in range(STEPS + 2):
                if a in fulls_at:
                    take_projection(fulls_at[a])
                if a - 1 in values_at:
                    take_values(values_at[a - 1])
                for kind, b, c in events.get(a - 1, []):
                    if kind == "tokens":
                        continue
                    dve.wait_ge(t_ready, t_index[(kind, b, c)] + 1)
                    if kind == "max":
                        dve.wait_ge(nm_done, 2 * b + 1)
                        dve.scalar_tensor_tensor(nm[:, b % 2, 1, :], bank[7][0:H, 0:T], -1.0, nm[:, b % 2, 0, :].bitcast(F32),
                                                 ALU.mult, ALU.subtract).then_inc(nm_done, 1)
                    elif kind == "out":
                        src = bank[7].rearrange("p (h r) -> p h r", r=32)
                        link(dve.reciprocal(rz[:, :], src[:, :, D]))
                        dve.scalar_tensor_tensor(o_n[:, c, :].rearrange("p (h d) -> p h d", d=D), src[:, :, 0:D],
                                                 mask_c[:, b * TC + c:b * TC + c + 1],
                                                 rz[:, :].rearrange("p (h o) -> p h o", o=1).to_broadcast([P, H, D]),
                                                 ALU.mult, ALU.mult).then_inc(on_done, 1)
                    elif kind == "router":
                        lg = bank[7][:, 0:E]
                        link(dve.max(v8[:, b, :], lg))
                        dve.max_index(i8[:, b, :], v8[:, b, :], lg).then_inc(top_done, 1)
                    else:
                        dve.scalar_tensor_tensor(x_sb[:, b, :], bank[7][:, 0:T], tg[:, 0:1], x_sb[:, b, :],
                                                 ALU.mult, ALU.add).then_inc(x1_done, 1)
                b, phase = divmod(a - BACK - 4, 16)
                if phase == 0 and 0 <= b < B:
                    dve.wait_ge(rstd2_done, b + 1)
                    normalize([b], tok_normed)
                if a < NA:
                    dve.wait_ge(a_done, a + 1)
                    b, h = divmod(a, H)
                    if b >= 2 and h == 0:
                        dve.wait_ge(t_ready, t_index[("max", b - 2, 0)] + 1)
                    dve.tensor_reduce(mx[:, b % 2, :, h], bank[a % 2].rearrange("p (c s) -> p c s", c=TC),
                                      AX.X, ALU.max).then_inc(max_done, 1)
                b, phase = divmod(a - BACK - 1, 16)
                if phase == 0 and 0 <= b < B:
                    dve.wait_ge(x1_done, b + 1)
                    link(dve.bn_stats(stats[:, b, :], x_sb[:, b, :]))
                    link(dve.bn_aggr(mv[:, b, :], stats[:, b, :]))
                    dve.tensor_scalar(var[:, b:b + 1], mv[:, b, 1:2], EPS, None, ALU.add).then_inc(var2_done, 1)
                if a - 3 in up_at:
                    shared_hidden(up_at[a - 3])
                if a == DOWNS + 5:
                    for b in range(2):
                        shared_add(b)

            dve.tensor_tensor(e6[:, :, :], v8[:, :, 0:K], v8[:, :, 0:1].to_broadcast([P, B, K]), ALU.subtract).then_inc(soft, 1)
            dve.wait_ge(consts, 9)
            dve.wait_ge(far_done, B - 1)
            ranks(dve, link, B - 1)
            dve.wait_ge(far_done, B)
            dve.wait_ge(pos_ready, 1)
            dve.tensor_tensor(route[:, :, :, 0], bank[7].rearrange("p (b e) -> p b e", b=B), far[:, :, :], ALU.add).then_inc(route_done, 1)
            def weights():
                dve.wait_ge(softd, 1)
                link(dve.tensor_reduce(e6s[:, :], e6[:, :, :], AX.X, ALU.add))
                link(dve.reciprocal(e6s[:, :], e6s[:, :]))
                link(dve.tensor_scalar(e6s[:, :], e6s[:, :], tg[:, 2:3], None, ALU.mult))
                dve.tensor_tensor(ww[:, :, :], e6[:, :, :], e6s[:, :].rearrange("p (b o) -> p b o", o=1).to_broadcast([P, B, K]), ALU.mult).then_inc(weights_done, 1)

            def extra_tiles(_):
                dve.wait_ge(cnt_ready, 1)
                link(dve.tensor_copy(n_e[:, :], bank[2][0:E, 0:1]))
                link(dve.tensor_scalar(c_tmp[:, :], c128[:, :], n_e[:, 0:1], None, ALU.is_lt))
                dve.tensor_reduce(extra[:, :], c_tmp[:, :], AX.X, ALU.add).then_inc(beg_in, 1)

            def spans(_):
                dve.wait_ge(beg_ready, 1)
                link(dve.tensor_copy(o_beg[:, :], bank[2][0:E, 8:9]))
                link(dve.tensor_tensor(o_end[:, :], o_beg[:, :], extra[:, :], ALU.add))
                link(dve.tensor_scalar(t_ge[:, :], iota_q[:, :], o_beg[:, 0:1], None, ALU.is_ge))
                link(dve.scalar_tensor_tensor(t_in[:, :], iota_q[:, :], o_end[:, 0:1], t_ge[:, :], ALU.is_lt, ALU.mult))
                link(dve.tensor_scalar(t_c[:, :], iota_q[:, :], o_beg[:, 0:1], 1.0 - B, ALU.subtract, ALU.add))
                dve.tensor_tensor(t_c2[:, :], t_c[:, :], t_in[:, :], ALU.mult).then_inc(plan_in, 1)

            def take_plan(_):
                dve.wait_ge(plan_ready, 1)
                src = bank[2][0:1, 16:16 + 2 * NOV + 1]
                dve.tensor_copy(plan[0:1, 0:NOV], src[:, 0:NOV])
                dve.tensor_scalar(plan[0:1, NOV:2 * NOV], src[:, NOV:2 * NOV], float(B), None, ALU.add)
                dve.tensor_copy(plan[0:1, 2 * NOV:2 * NOV + 1], src[:, 2 * NOV:2 * NOV + 1]).then_inc(plan_done, 1)

            chunks = []

            def load_plan(_):
                dve.wait_ge(plan_done, 1)
                chunks.extend(dve.value_load(plan[0:1, NOV + i:NOV + i + 1], min_val=0, max_val=B) for i in range(OVER))

            def hot_rows(e):
                dve.wait_ge(pick_done, e.v + 1)
                if not first(e, 2):
                    dve.wait_ge(inv, e.v - 1)
                base = chunks[e.v - E] * P if isinstance(e.v, int) and e.v >= E else 0
                dve.tensor_tensor(onehot[:, e.r % 2, :, :],
                                  iota_w[:, bass.ds(base, P)].rearrange("p (o j) -> p o j", o=1).to_broadcast([P, B, P]),
                                  picked[:, e.r % 4, :, 0:1].to_broadcast([P, B, P]), ALU.is_equal).then_inc(hot, 1)

            def indices(e):
                dve.wait_ge(inv, e.v + 1)
                if not first(e, 8):
                    dve.wait_ge(y_out[e.r % 4], 16 * (e.use(4) - 1))
                src = bank[7 * (e.r % 2)][:, 0:3]
                dve.tensor_copy(g_idx[:, e.r:e.r + 1], src[:, 0:1])
                dve.tensor_scalar(s_idx[:, e.r:e.r + 1], src[:, 1:2], float(FAR), src[:, 2:3],
                                  ALU.add, ALU.add).then_inc(idx, 1)

            def hidden(e):
                dve.wait_ge(th_done, e.v + 1)
                if not first(e, 2):
                    dve.wait_ge(s2, e.v - 1)
                dve.scalar_tensor_tensor(hs[:, e.r % 2, :, :].rearrange("p c n -> p (c n)"), th[:, e.r % 2, :], 1.0,
                                         bank[3 + e.r % 2][0:IC, 0:2 * P], ALU.add, ALU.mult).then_inc(hs_done, 1)

            dve.wait_ge(route_done, 1)
            experts(dve, [(L_HOT, hot_rows), (L_IDX, indices), (L_S1, hidden)],
                    {"use": shared_hidden, "add": shared_add, "extra": extra_tiles, "spans": spans,
                     "take": take_plan, "load": load_plan})
            n_over = dve.value_load(plan[0:1, 2 * NOV:2 * NOV + 1], min_val=0, max_val=NOV)
            for r in range(4):
                dve.wait_ge(y_out[r], 16 * ((TILES - r + 3) // 4))
            with dve.If(n_over > OVER):
                with dve.Fori(0, n_over - OVER) as i:
                    c = dve.value_load(plan[0:1, bass.ds(i + (NOV + OVER), 1)], min_val=1, max_val=7)
                    dve.wait_ge(v_pick, i + 1)
                    dve.tensor_tensor(onehot[:, 0, :, :],
                                      iota_w[:, bass.ds(c * P, P)].rearrange("p (o j) -> p o j", o=1).to_broadcast([P, B, P]),
                                      picked[:, 0, :, 0:1].to_broadcast([P, B, P]), ALU.is_equal).then_inc(v_hot, 1)
                    dve.wait_ge(v_inv, i + 1)
                    dve.wait_ge(v_free, i + 1)
                    src = bank[0][:, 0:3]
                    dve.tensor_copy(g_idx[:, 0:1], src[:, 0:1])
                    dve.tensor_scalar(s_idx[:, 0:1], src[:, 1:2], float(FAR), src[:, 2:3],
                                      ALU.add, ALU.add).then_inc(v_idx, 1)
                    dve.wait_ge(v_th, i + 1)
                    dve.scalar_tensor_tensor(hs[:, 0, :, :].rearrange("p c n -> p (c n)"), th[:, 0, :], 1.0,
                                             bank[3][0:IC, 0:2 * P], ALU.add, ALU.mult).then_inc(v_hs, 1)
            with dve.Else():
                dve.nop()
            weights()
            dve.wait_ge(weights_done, 1)
            for b in range(B):
                if b not in ON_PE:
                    dve.wait_ge(y6_in[b], 16)
                    for k in range(K):
                        ins = dve.scalar_tensor_tensor(x_sb[:, b, :], y6[:, b, k, :], ww[:, b, k:k + 1], x_sb[:, b, :],
                                                       ALU.mult, ALU.add)
                        if k < K - 1:
                            link(ins)
                    ins.then_inc(mixed[0], 1)

        @block.tensor
        def _(pe):
            mm = nc.tensor.matmul
            tr = nc.tensor.transpose

            def t_taken(kind, b, c):
                return {"max": (nm_done, 2 * (b + 1)), "out": (on_done, 2 * b + c + 1), "back": (x1_done, b + 1),
                        "tokens": (xt_done, b + 1), "router": (top_done, b + 1)}[kind]

            pe.wait_ge(ld_ctx, 16)
            pe.wait_ge(ld_w, 48)
            for j in range(B):
                k_side, c = j % 2 == 0, 2 * (j // 2)
                if not k_side:
                    pe.wait_ge(normed, c + 2)
                if j == 1:
                    pe.wait_ge(consts, 9)
                    pe.wait_ge(ld_mask, 32)
                    tr(bank[7][:, 0:B * TC], mask_r[:, :], ident[0:B * TC, 0:B * TC]).then_inc(mask_turned, 1)
                if j == 7:
                    pe.wait_ge(mask_col, 1)
                src = (ctx_sb if k_side else xn)[:, c:c + 2, :].rearrange("p b t -> p (b t)")
                mm(bank[j], w_sb[:, 0 if k_side else 1, :], src, start=True, stop=True).then_inc(proj, 1)
            def project_values(j):
                pe.wait_ge(fulls, j + 3)
                for s in range(4):
                    b, c = divmod(4 * j + s, TC)
                    last = mm(bank[j + 2][:, s * P:(s + 1) * P], ctx_sb[:, b, c * P:(c + 1) * P], w_sb[:, 2, :],
                              start=True, stop=True)
                last.then_inc(proj, 1)

            for j in range(VALUES):
                project_values(j)

            def shared_up(j):
                nb, c = divmod(j, 4)
                pe.wait_ge(ld_shared, 32)
                pe.wait_ge(xt_done, 4 * (nb + 1))
                if j < 4:
                    pe.wait_ge(max_done, NA)
                    if j:
                        pe.wait_ge(sh_done, j)
                elif j >= 6:
                    pe.wait_ge(sh_done, j - 1)
                for half in range(2):
                    for k in range(TC):
                        last = mm(bank[up_bank(j) + half][0:IC, :], sgu_sb[:, k, 4 * half + c, :],
                                  xt[:, k, nb * 512:(nb + 1) * 512], start=(k == 0), stop=(k == TC - 1))
                last.then_inc(sg_ready, 1)

            def shared_down(b):
                pe.wait_ge(sh_done, 4 * (b // 4 + 1))
                if b == 2:
                    pe.wait_ge(plan_done, 1)
                    pe.wait_ge(acc_done, 2)
                elif b >= 4:
                    pe.wait_ge(acc_done, b - 1)
                for c in range(4):
                    last = mm(bank[down_bank(b)][:, 0:T], s_h[:, c, b * P:(b + 1) * P], sd_sb[:, c, :],
                              start=(c == 0), stop=(c == 3))
                last.then_inc(sdn_ready, 1)
                if b == B - 1:
                    pe.wait_ge(acc_done, B)

            t_last = None
            for a in range(STEPS):
                if a < NA:
                    b, h = divmod(a, H)
                    if h == 0:
                        pe.wait_ge(stack_in[b % 3], 80 * (b // 3 + 1))
                    if a >= 2:
                        pe.wait_ge(max_done, a - 1)
                    for c in range(TC):
                        last = mm(bank[a % 2][:, c * T:(c + 1) * T], q_st[b % 3][0:AROWS, h, c * P:(c + 1) * P],
                                  k_st[b % 3][0:AROWS, h, :], start=True, stop=True)
                    last.then_inc(a_done, 1)
                if a in values_at:
                    project_values(values_at[a])
                p = pair_of(a)
                if p is not None:
                    b, h = divmod(2 * p, H)
                    if h == 0:
                        pe.wait_ge(max_in, 32 * (b + 1))
                        pe.wait_ge(ones_in, 48)
                        pe.wait_ge(taken, 4)
                    if p >= 2:
                        pe.wait_ge(exp_done, p - 1)
                    for i in range(2):
                        for c in range(TC):
                            o = (i * TC + c) * T
                            last = mm(score[p % 2][:, o:o + T], k_st[b % 3][0:BROWS, h + i, c * P:(c + 1) * P],
                                      q_st[b % 3][0:BROWS, h + i, :], start=True, stop=True)
                    last.then_inc(b_done, 1)
                for c in range(TC):
                    gq = group_of(a - c)
                    if gq is None:
                        continue
                    b, g = divmod(gq, 4)
                    if c == 0:
                        pe.wait_ge(exp_done, 2 * gq + 2)
                        if gq >= 1:
                            pe.wait_ge(os_done, gq)
                        if g == 0:
                            pe.wait_ge(v_ready, b + 1)
                    for i in range(4):
                        pr = probs[:, (2 * gq + i // 2) % 4, :].rearrange("p (i c t) -> p i c t", i=2, c=TC)
                        last = mm(bank[6][32 * i:32 * i + 32, 0:T], v_pad[:, b % 2, c, 4 * g + i, :],
                                  pr[:, i % 2, c, :], start=(c == 0), stop=(c == TC - 1))
                    if c == TC - 1:
                        last.then_inc(pv_done, 1)
                for kind, b, c in events.get(a, []):
                    if t_last is not None:
                        pe.wait_ge(*t_taken(*t_last))
                    t_last = (kind, b, c)
                    if kind == "max":
                        pe.wait_ge(max_done, 16 * (b + 1))
                        for i in range(TC):
                            last = tr(bank[7][0:H, i * P:(i + 1) * P], mx[:, b % 2, i, :], ident[:, :])
                    elif kind == "out":
                        pe.wait_ge(os_done, 4 * (b + 1))
                        for g in range(4):
                            last = tr(bank[7][:, g * P:(g + 1) * P], o_sb[:, b % 2, g, c * P:(c + 1) * P], ident[:, :])
                    elif kind == "back":
                        pe.wait_ge(on_done, 2 * (b + 1))
                        for i in range(TC):
                            last = tr(bank[7][:, i * P:(i + 1) * P], o_n[:, i, :], ident[:, :])
                    elif kind == "tokens":
                        pe.wait_ge(tok_normed, b + 1)
                        for k in range(TC):
                            last = tr(bank[7][:, k * P:(k + 1) * P], xn[:, b, k * P:(k + 1) * P], ident[:, :])
                    else:
                        pe.wait_ge(ld_gate, 16)
                        pe.wait_ge(xt_done, b + 1)
                        for k in range(TC):
                            last = mm(bank[7][:, 0:E], xt[:, k, b * P:(b + 1) * P], gate_sb[:, k, :],
                                      start=(k == 0), stop=(k == TC - 1))
                    last.then_inc(t_ready, 1)
                if a in up_at:
                    shared_up(up_at[a])
                if a == DOWNS:
                    for b in range(2):
                        shared_down(b)

            pe.wait_ge(exp_done, NP)
            pe.wait_ge(os_done, NG)
            shared_up(4)
            pe.wait_ge(top_done, B)
            pe.wait_ge(chosen_done, B)
            for b in range(B):
                for b2 in range(b + 1):
                    last = mm(bank[7][:, b * E:(b + 1) * E], (tri if b2 == b else ones16)[:, :], chosen[:, b2, :],
                              start=(b2 == 0), stop=(b2 == b))
            last.then_inc(pos_ready, 1)
            for b in range(B):
                last = mm(bank[2][0:E, 0:1], chosen[:, b, :], ones16[:, 0:1], start=(b == 0), stop=(b == B - 1))
            last.then_inc(cnt_ready, 1)

            def begins(_):
                pe.wait_ge(beg_in, 1)
                mm(bank[2][0:E, 8:9], tri_f[:, :], extra[:, :], start=True, stop=True).then_inc(beg_ready, 1)

            def make_plan(_):
                pe.wait_ge(plan_in, 1)
                mm(bank[2][0:1, 16:16 + NOV], iota_p[0:E, :], t_in[:, :], start=True, stop=True)
                mm(bank[2][0:1, 16 + NOV:16 + 2 * NOV], ones_f[:, :], t_c2[:, :], start=True, stop=True)
                mm(bank[2][0:1, 16 + 2 * NOV:17 + 2 * NOV], ones_f[:, :], extra[:, :], start=True, stop=True).then_inc(plan_ready, 1)

            def invert(e):
                pe.wait_ge(hot, e.v + 1)
                if not first(e, 2):
                    pe.wait_ge(idx, e.v - 1)
                for b in range(B):
                    last = mm(bank[7 * (e.r % 2)][:, 0:3], onehot[:, e.r % 2, b, :], picked[:, e.r % 4, b, 1:4],
                              start=(b == 0), stop=(b == B - 1))
                last.then_inc(inv, 1)

            def transpose_rows(e):
                pe.wait_ge(rows_in[e.r % 4], 16 * (e.use(4) + 1))
                if not first(e, 2):
                    pe.wait_ge(xe_done, e.v - 1)
                for k in range(TC):
                    last = tr(bank[1 + e.r % 2][:, k * P:(k + 1) * P], rows[:, e.r % 4, k * P:(k + 1) * P], ident[:, :])
                last.then_inc(xpose, 1)

            def first_product(e):
                pe.wait_ge(w_in[e.r % 4], 32 * (e.use(4) + 1))
                pe.wait_ge(xe_done, e.v + 1)
                if not first(e, 2):
                    pe.wait_ge(hs_done, e.v - 1)
                for c in range(2):
                    for k in range(TC):
                        last = mm(bank[3 + e.r % 2][0:IC, c * P:(c + 1) * P], w1_sb[:, e.r % 4, k, c * IC:(c + 1) * IC],
                                  xe[:, e.r % 2, k, :], start=(k == 0), stop=(k == TC - 1))
                last.then_inc(s1, 1)

            def second_product(e):
                pe.wait_ge(hs_done, e.v + 1)
                if not first(e, 2):
                    pe.wait_ge(y_done, e.v - 1)
                for c in range(2):
                    last = mm(bank[5 + e.r % 2][:, 0:T], hs[:, e.r % 2, c, :], w2_sb[0:IC, e.r % 4, c, :],
                              start=(c == 0), stop=(c == 1))
                last.then_inc(s2, 1)

            experts(pe, [(0, second_product), (L_S1, first_product), (L_X, transpose_rows), (L_INV, invert)],
                    {"up": shared_up, "down": shared_down, "begins": begins, "plan": make_plan})
            n_over = pe.value_load(plan[0:1, 2 * NOV:2 * NOV + 1], min_val=0, max_val=NOV)
            pe.wait_ge(y_done, TILES)
            pe.sem_inc(v_s2, 1)
            with pe.If(n_over > OVER):
                with pe.Fori(0, n_over - OVER) as i:
                    pe.wait_ge(v_hot, i + 1)
                    for b in range(B):
                        last = mm(bank[0][:, 0:3], onehot[:, 0, b, :], picked[:, 0, b, 1:4], start=(b == 0), stop=(b == B - 1))
                    last.then_inc(v_inv, 1)
                    pe.wait_ge(v_rows, 16 * i + 16)
                    for k in range(TC):
                        last = tr(bank[1][:, k * P:(k + 1) * P], rows[:, 0, k * P:(k + 1) * P], ident[:, :])
                    last.then_inc(v_x, 1)
                    pe.wait_ge(v_w, 32 * i + 32)
                    pe.wait_ge(v_xe, i + 1)
                    for c in range(2):
                        for k in range(TC):
                            last = mm(bank[3][0:IC, c * P:(c + 1) * P], w1_sb[:, 0, k, c * IC:(c + 1) * IC],
                                      xe[:, 0, k, :], start=(k == 0), stop=(k == TC - 1))
                    last.then_inc(v_s1, 1)
                    pe.wait_ge(v_hs, i + 1)
                    pe.wait_ge(v_free, i + 1)
                    for c in range(2):
                        last = mm(bank[5][:, 0:T], hs[:, 0, c, :], w2_sb[0:IC, 0, c, :], start=(c == 0), stop=(c == 1))
                    last.then_inc(v_s2, 1)
            with pe.Else():
                pe.nop()
            for n, b in enumerate(ON_PE):
                pe.wait_ge(weighted, n + 1)
                if n >= 2:
                    pe.wait_ge(mixed[1], n - 1)
                for k in range(K + 1):
                    last = mm(bank[n % 2][:, 0:T], ident[:, :], y6[:, b, k, :] if k < K else x_sb[:, b, :],
                              start=(k == 0), stop=(k == K))
                last.then_inc(summed, 1)


def kernel(**inputs):
    import numpy as np
    import concourse.bacc as bacc
    from concourse.bass_utils import run_bass_kernel_spmd as run

    P, H, D, IC = 128, 16, 8, 96
    a = {k: np.asarray(v) for k, v in inputs.items()}
    by_width = np.arange(H * D).reshape(H, D).T.reshape(-1)

    def pad(w, axis, size):
        width = [(0, 0)] * w.ndim
        width[axis] = (0, size - w.shape[axis])
        return np.pad(w, width)

    E, I, T = a["L0_ffn_experts_w1"].shape
    half = I // 2
    w1 = pad(a["L0_ffn_experts_w1"].reshape(E, 2, half, T // P, P), 2, IC)
    w2 = pad(a["L0_ffn_experts_w2"].reshape(E, T, 2, half), 3, IC)
    sgu = pad(a["L0_ffn_shared_gate_up"].reshape(8, half, T // P, P), 1, IC)
    sd = pad(a["L0_ffn_shared_down"].reshape(T, 4, half), 2, IC)
    laid = {
        "x": a["x"].transpose(1, 0, 2), "ctx": a["ctx_2048"].transpose(1, 0, 2), "mask": a["mask_Bx1x2048_fk1"][:, 0],
        "g_xattn": a["g_xattn"][None], "g_ffn": a["g_ffn"][None],
        "wq": a["L0_xattn_Wq"][by_width].T, "bq": a["L0_xattn_bq"][by_width][:, None],
        "wk": a["L0_xattn_Wk"][by_width].T, "bk": a["L0_xattn_bk"][by_width][:, None],
        "wv": a["L0_xattn_Wv"].T, "bv": a["L0_xattn_bv"][None],
        "gate": a["L0_ffn_gate_w"].T.reshape(T // P, P, E).transpose(1, 0, 2),
        "w1": w1.transpose(0, 4, 3, 1, 2).reshape(E, P, T // P, 2 * IC),
        "w2": w2.transpose(0, 3, 2, 1),
        "sgu": sgu.transpose(3, 2, 0, 1), "sd": sd.transpose(2, 1, 0),
    }
    nc = bacc.Bacc("TRN2", target_bir_lowering=False, num_devices=1)
    arrays, args = {}, []
    for name, w in laid.items():
        w = np.ascontiguousarray(w)
        arrays[f"in_{name}"] = w
        args.append(nc.dram_tensor(f"in_{name}", w.shape, mybir.dt.from_np(w.dtype), kind="ExternalInput").ap())
    out = nc.dram_tensor("out", (P, a["x"].shape[0], T), mybir.dt.float32, kind="ExternalOutput").ap()
    build_gated_block(nc, *args, out)
    r = run(nc, [arrays], core_ids=[0])
    return np.ascontiguousarray(np.asarray(r.results[0]["out"]).transpose(1, 0, 2))
```
